# Optimizing a Trainium2 kernel written in Bass

```python
import numpy as np
import jax
import jax.numpy as jnp

def _softmax(x, axis=-1):
    return jax.nn.softmax(x, axis=axis)

def _gelu(x):
    return jax.nn.gelu(x, approximate=True)

def _silu(x):
    return jax.nn.silu(x)

def _sigmoid(x):
    return jax.nn.sigmoid(x)

def _layernorm(x, axis=-1, eps=1e-05):
    m = jnp.mean(x, axis=axis, keepdims=True)
    v = jnp.var(x, axis=axis, keepdims=True)
    return (x - m) / jnp.sqrt(v + eps)

def _scatter_add(tgt, idx, src, axis=0):
    return tgt.at[idx].add(src)

def _segment_sum(src, seg, n):
    return jax.ops.segment_sum(src, seg, n)
kernel_name = 'mk_adj_ffn_d2_adj_r2_8d6247'

def setup_inputs(seed: int=0):
    np.random.seed(seed)
    _w = jnp.asarray

    def _rec_inputs():
        import jax
        import jax.numpy as jnp
        _gk = jax.random.key(seed)
        x = -0.0005207 + 1.001 * jax.random.normal(jax.random.fold_in(_gk, 1), (2048, 128), jnp.float32)
        _w = (1.0 + jnp.arange(2048, dtype=jnp.float32)) ** (-0.5)
        _w = _w / _w.mean()
        _pij = jnp.clip(0.000976562 * _w[:, None] * _w[None, :], 0.0, 1.0)
        _a = jax.random.uniform(jax.random.fold_in(_gk, 2), (2048, 2048)) < _pij
        _a = jnp.logical_or(_a, jnp.eye(2048, dtype=bool))
        _af = _a.astype(jnp.float32)
        _af = _af * jax.random.uniform(jax.random.fold_in(_gk, 3), (2048, 2048), jnp.float32, 0.05, 1)
        adj = _af
        return (x, adj)
    x, adj = _rec_inputs()

    def _L0_gnn_setup():
        import jax, jax.numpy as jnp
        import numpy as np
        N, IN_C, OUT_C = (4096, 128, 128)
        key = jax.random.key(seed)
        k1, k2, k3 = jax.random.split(key, 3)
        x = jax.random.normal(k1, (N, IN_C), dtype=jnp.float32)
        adj = jax.random.uniform(k2, (N, N), dtype=jnp.float32)
        w = jax.random.uniform(k3, (IN_C, OUT_C), dtype=jnp.float32)
        return {'x': x, 'adj': adj, 'w': w}
    _L0_gnn_all = _L0_gnn_setup()
    _L0_gnn_in = {k: v for k, v in _L0_gnn_all.items() if k in ('w',)}
    del _L0_gnn_all

    def _L0_ffn_setup():
        import jax, jax.numpy as jnp
        import numpy as np
        B, S, H, F, E, K = (8, 2048, 128, 256, 16, 2)
        EPS = 1e-05
        key = jax.random.key(seed)
        ks = jax.random.split(key, 9)
        sc = 0.02
        return {'x': jax.random.normal(ks[0], (B, S, H), dtype=jnp.float32), 'gate_w': jax.random.normal(ks[1], (H, E), dtype=jnp.float32) * sc, 'gate_b': jnp.zeros((E,), dtype=jnp.float32), 'w1': jax.random.normal(ks[2], (E, H, F), dtype=jnp.float32) * sc, 'b1': jnp.zeros((E, F), dtype=jnp.float32), 'w2': jax.random.normal(ks[3], (E, F, H), dtype=jnp.float32) * sc, 'b2': jnp.zeros((E, H), dtype=jnp.float32), 'gamma': jnp.ones((H,), dtype=jnp.float32), 'beta': jnp.zeros((H,), dtype=jnp.float32)}
    _L0_ffn_all = _L0_ffn_setup()
    _L0_ffn_in = {k: v for k, v in _L0_ffn_all.items() if k in ('gate_w', 'gate_b', 'w1', 'b1', 'w2', 'b2', 'gamma', 'beta')}
    del _L0_ffn_all

    def _L1_gnn_setup():
        import jax, jax.numpy as jnp
        import numpy as np
        N = 3072
        HID = 128
        T = 350
        DENSITY = 0.05
        key = jax.random.key(seed)
        k1, k2, k3, k4, k5, k6 = jax.random.split(key, 6)
        h = jax.random.normal(k1, (N, HID), dtype=jnp.float32)
        a = jax.random.uniform(k2, (N, N), dtype=jnp.float32)
        mask = jax.random.uniform(k3, (N, N)) < DENSITY
        adj = jnp.where(mask, a, 0.0)
        simlar = jax.random.normal(k4, (N, N), dtype=jnp.float32)
        s = 1.0 / np.sqrt(HID)
        W_proj = jax.random.uniform(k5, (HID, HID), minval=-s, maxval=s, dtype=jnp.float32)
        b_proj = jnp.zeros((HID,), dtype=jnp.float32)
        W_gcn = jax.random.uniform(k6, (HID, HID), minval=-s, maxval=s, dtype=jnp.float32)
        b_gcn = jnp.zeros((HID,), dtype=jnp.float32)
        return {'h': h, 'adj': adj, 'simlar': simlar, 'W_proj': W_proj, 'b_proj': b_proj, 'W_gcn': W_gcn, 'b_gcn': b_gcn}
    _L1_gnn_all = _L1_gnn_setup()
    _L1_gnn_in = {k: v for k, v in _L1_gnn_all.items() if k in ('W_proj', 'b_proj', 'W_gcn', 'b_gcn')}
    del _L1_gnn_all

    def _L1_ffn_setup():
        import jax, jax.numpy as jnp
        import numpy as np
        D_MODEL = 128
        N_EXPERTS = 16
        HIDDEN = 256
        SCALE = 0.02
        key = jax.random.key(seed)
        ks = jax.random.split(key, 5)
        x = jax.random.normal(ks[0], (4, 4096, D_MODEL), dtype=jnp.float32)
        gate_w = jax.random.normal(ks[1], (D_MODEL, N_EXPERTS), dtype=jnp.float32) * SCALE
        gate_b = jnp.zeros((N_EXPERTS,), dtype=jnp.float32)
        w1 = jax.random.normal(ks[2], (N_EXPERTS, D_MODEL, HIDDEN), dtype=jnp.float32) * SCALE
        w2 = jax.random.normal(ks[3], (N_EXPERTS, D_MODEL, HIDDEN), dtype=jnp.float32) * SCALE
        w3 = jax.random.normal(ks[4], (N_EXPERTS, HIDDEN, D_MODEL), dtype=jnp.float32) * SCALE
        return {'x': x, 'gate_w': gate_w, 'gate_b': gate_b, 'w1': w1, 'w2': w2, 'w3': w3}
    _L1_ffn_all = _L1_ffn_setup()
    _L1_ffn_in = {k: v for k, v in _L1_ffn_all.items() if k in ('gate_w', 'gate_b', 'w1', 'w2', 'w3')}
    del _L1_ffn_all
    return {'x': x, 'adj': adj, 'L0_gnn_w': _L0_gnn_in['w'], 'L0_ffn_gate_w': _L0_ffn_in['gate_w'], 'L0_ffn_gate_b': _L0_ffn_in['gate_b'], 'L0_ffn_w1': _L0_ffn_in['w1'], 'L0_ffn_b1': _L0_ffn_in['b1'], 'L0_ffn_w2': _L0_ffn_in['w2'], 'L0_ffn_b2': _L0_ffn_in['b2'], 'L0_ffn_gamma': _L0_ffn_in['gamma'], 'L0_ffn_beta': _L0_ffn_in['beta'], 'L1_gnn_W_proj': _L1_gnn_in['W_proj'], 'L1_gnn_b_proj': _L1_gnn_in['b_proj'], 'L1_gnn_W_gcn': _L1_gnn_in['W_gcn'], 'L1_gnn_b_gcn': _L1_gnn_in['b_gcn'], 'L1_ffn_gate_w': _L1_ffn_in['gate_w'], 'L1_ffn_gate_b': _L1_ffn_in['gate_b'], 'L1_ffn_w1': _L1_ffn_in['w1'], 'L1_ffn_w2': _L1_ffn_in['w2'], 'L1_ffn_w3': _L1_ffn_in['w3']}

def reference(x, adj, L0_gnn_w, L0_ffn_gate_w, L0_ffn_gate_b, L0_ffn_w1, L0_ffn_b1, L0_ffn_w2, L0_ffn_b2, L0_ffn_gamma, L0_ffn_beta, L1_gnn_W_proj, L1_gnn_b_proj, L1_gnn_W_gcn, L1_gnn_b_gcn, L1_ffn_gate_w, L1_ffn_gate_b, L1_ffn_w1, L1_ffn_w2, L1_ffn_w3):
    import jax
    import jax.numpy as jnp

    def _L0_gnn_ref(x, adj, w):
        import jax, jax.numpy as jnp
        import numpy as np
        N, IN_C, OUT_C = (4096, 128, 128)
        A = adj + jnp.eye(adj.shape[0], dtype=adj.dtype)
        deg = jnp.sum(A, axis=1)
        d_isqrt = jax.lax.rsqrt(deg)
        A_hat = A * d_isqrt[:, None] * d_isqrt[None, :]
        h = jnp.matmul(A_hat, x)
        return jax.nn.elu(jnp.matmul(h, w))

    def _L0_ffn_ref(x, gate_w, gate_b, w1, b1, w2, b2, gamma, beta):
        import jax, jax.numpy as jnp
        import numpy as np
        B, S, H, F, E, K = (8, 2048, 128, 256, 16, 2)
        EPS = 1e-05
        gate_logits = x @ gate_w + gate_b
        topk_vals, topk_idx = jax.lax.top_k(gate_logits, K)
        topk_w = jax.nn.softmax(topk_vals, axis=-1)
        h = jax.nn.relu(jnp.einsum('bsh,ehf->bsef', x, w1) + b1)
        expert_out = jnp.einsum('bsef,efh->bseh', h, w2) + b2
        sel = jnp.take_along_axis(expert_out, topk_idx[:, :, :, None], axis=2)
        moe = jnp.sum(topk_w[..., None] * sel, axis=2)
        y = x + moe
        mu = jnp.mean(y, axis=-1, keepdims=True)
        var = jnp.var(y, axis=-1, keepdims=True)
        return (y - mu) / jnp.sqrt(var + EPS) * gamma + beta

    def _L1_gnn_ref(h, adj, simlar, W_proj, b_proj, W_gcn, b_gcn):
        import jax, jax.numpy as jnp
        import numpy as np
        N = 3072
        HID = 128
        T = 350
        DENSITY = 0.05
        sim = jnp.tanh(adj * simlar)
        filt = sim * (adj > 0).astype(sim.dtype)
        vals, idx = jax.lax.top_k(filt, T)
        nnz = jnp.sum(filt != 0, axis=1)
        keep = jnp.arange(T)[None, :] < nnz[:, None]
        rows = jnp.arange(filt.shape[0])[:, None]
        new_adj = jnp.zeros_like(filt).at[rows, idx].set(jnp.where(keep, vals, 0.0))
        h2 = jnp.tanh(h @ W_proj + b_proj)
        feat = jax.nn.relu(new_adj @ (h2 @ W_gcn) + b_gcn)
        return feat

    def _L1_ffn_ref(x, gate_w, gate_b, w1, w2, w3):
        import jax, jax.numpy as jnp
        import numpy as np
        D_MODEL = 128
        N_EXPERTS = 16
        HIDDEN = 256
        SCALE = 0.02
        n_experts = w1.shape[0]
        logits = jnp.einsum('bsd,de->bse', x, gate_w) + gate_b
        probs = jax.nn.softmax(logits, axis=-1)
        top_probs, top_idx = jax.lax.top_k(probs, 2)
        top_probs = top_probs / jnp.sum(top_probs, axis=-1, keepdims=True)
        dispatch = jnp.sum(jax.nn.one_hot(top_idx, n_experts, dtype=x.dtype) * top_probs[..., None], axis=-2)
        h1 = jnp.einsum('bsd,edh->bseh', x, w1)
        h2 = jnp.einsum('bsd,edh->bseh', x, w2)
        hidden = jax.nn.silu(h1) * h2
        expert_out = jnp.einsum('bseh,eho->bseo', hidden, w3)
        return jnp.einsum('bseo,bse->bso', expert_out, dispatch)
    x = x + _L0_gnn_ref(_layernorm(x, axis=-1), adj, L0_gnn_w)
    x = x + _L0_ffn_ref(_layernorm(x, axis=-1)[None], L0_ffn_gate_w, L0_ffn_gate_b, L0_ffn_w1, L0_ffn_b1, L0_ffn_w2, L0_ffn_b2, L0_ffn_gamma, L0_ffn_beta)[0]
    x = x + _L1_gnn_ref(_layernorm(x, axis=-1), adj, adj, L1_gnn_W_proj, L1_gnn_b_proj, L1_gnn_W_gcn, L1_gnn_b_gcn)
    x = x + _L1_ffn_ref(_layernorm(x, axis=-1)[None], L1_ffn_gate_w, L1_ffn_gate_b, L1_ffn_w1, L1_ffn_w2, L1_ffn_w3)[0]
    return x

_drawn_inputs = setup_inputs


def setup_inputs(seed=0):
    import zlib

    import numpy as np

    out = dict(_drawn_inputs(seed))
    spreads = {'L0_ffn_gate_b': (0.0, 0.378),
     'L0_ffn_b1': (0.0, 0.8),
     'L0_ffn_b2': (0.0, 0.345),
     'L0_ffn_gamma': (1.0, 0.2),
     'L0_ffn_beta': (0.0, 0.1),
     'L1_gnn_b_proj': (0.0, 0.66),
     'L1_gnn_b_gcn': (0.0, 0.391),
     'L1_ffn_gate_b': (0.0, 0.8)}
    factors = {'L0_ffn_w1': 5.591,
     'L0_ffn_w2': 4.372,
     'L1_ffn_gate_w': 8.0,
     'L1_ffn_w1': 8.0,
     'L1_ffn_w2': 8.0,
     'L1_ffn_w3': 8.0}
    for name, (base, spread) in spreads.items():
        noise = np.random.default_rng([zlib.crc32(name.encode()), seed]).standard_normal(out[name].shape)
        drawn = base * np.exp(spread * noise) if base else spread * noise
        out[name] = jnp.asarray(drawn.astype(out[name].dtype))
    for name, factor in factors.items():
        out[name] = (out[name] * factor).astype(out[name].dtype)
    return out
```

```python
import concourse.bass as bass
from concourse import mybir
from contextlib import ExitStack


class Count:

    def __init__(self, engine, sem):
        self.engine, self.sem, self.n = engine, sem, 0

    def inc(self, instruction):
        instruction.then_inc(self.sem, 1)
        self.n += 1

    def wait(self):
        self.engine.wait_ge(self.sem, self.n)


def gnn_moe_gnn_moe_kernel(
    nc: bass.Bass,
    x: bass.AP,
    adj: bass.AP,
    L0_gnn_w: bass.AP,
    L0_ffn_gate_w: bass.AP,
    L0_ffn_gate_b: bass.AP,
    L0_ffn_w1: bass.AP,
    L0_ffn_b1: bass.AP,
    L0_ffn_w2: bass.AP,
    L0_ffn_b2: bass.AP,
    L0_ffn_gamma: bass.AP,
    L0_ffn_beta: bass.AP,
    L1_gnn_W_proj: bass.AP,
    L1_gnn_b_proj: bass.AP,
    L1_gnn_W_gcn: bass.AP,
    L1_gnn_b_gcn: bass.AP,
    L1_ffn_gate_w: bass.AP,
    L1_ffn_gate_b: bass.AP,
    L1_ffn_w1: bass.AP,
    L1_ffn_w2: bass.AP,
    L1_ffn_w3: bass.AP,
    out: bass.AP,
):
    f32, bf16 = mybir.dt.float32, mybir.dt.bfloat16
    i32, u32 = mybir.dt.int32, mybir.dt.uint32
    ALU = mybir.AluOpType
    ACT = mybir.ActivationFunctionType
    AX = mybir.AxisListType.X

    P = 128
    N, D = x.shape
    E, _, F = L0_ffn_w1.shape
    NT = N // P
    GT = 4
    NG = NT // GT
    GW = GT * P
    K = 2
    TOP = 350
    EPS = 1e-5
    C = K * NT
    SLOTS = (K * N + E * (P - 1)) // P
    RING = 4
    FH = F // P

    ctx = ExitStack()
    with ctx:
        def sb(name, shape, dt=f32):
            return ctx.enter_context(nc.sbuf_tensor(name, shape, dt))

        def sem(name):
            return ctx.enter_context(nc.semaphore(name))

        adjT = sb("adjT", [P, NT, N])
        region = sb("region", [P, 10240])
        xres = sb("xres", [P, NT, D])
        xn = sb("xn", [P, NT, D])
        wide = sb("wide", [P, 2, GW])
        gath = sb("gath", [P, K, RING, D])
        slot_in = sb("slot_in", [P, RING, D])
        slotT = sb("slotT", [P, 2, P])
        hbuf = sb("hbuf", [P, 4, F])
        slot_out = sb("slot_out", [P, RING, D])
        ident = sb("ident", [P, P])
        before = sb("before", [P, P], bf16)
        ones = sb("ones", [P, P], bf16)
        segment = sb("segment", [P, E * C], bf16)
        iota_e = sb("iota_e", [P, E])
        iota_s = sb("iota_s", [1, SLOTS])
        gnn_w = sb("gnn_w", [P, D])
        proj_w = sb("proj_w", [P, D])
        gcn_w = sb("gcn_w", [P, D])
        proj_b = sb("proj_b", [P, 1])
        gcn_b = sb("gcn_b", [P, 1])
        gate_w = [sb(f"gate_w{n}", [P, E]) for n in range(2)]
        gate_b = [sb(f"gate_b{n}", [P, E]) for n in range(2)]
        gamma = sb("gamma", [P, D])
        beta = sb("beta", [P, D])
        b1T = sb("b1T", [P, FH, E])
        deg = sb("deg", [P, NT])
        dis = sb("dis", [P, NT])
        nnz = sb("nnz", [P, NT])
        over = sb("over", [P, NT])
        over_any = sb("over_any", [P, 1], bf16)
        flag = sb("flag", [1, 1], i32)
        stats = sb("stats", [P, GT, 6])
        mv = sb("mv", [P, NT, 2])
        rstd = sb("rstd", [P, NT])
        shift = sb("shift", [P, NT])
        chosen = sb("chosen", [P, K, NT])
        root_v = sb("root_v", [P, GT])
        root_t = sb("root_t", [P, GT])
        wexp = sb("wexp", [P, NT])
        wsum = sb("wsum", [P, NT])
        wk = sb("wk", [P, K, NT])
        count_i = sb("count_i", [P, E], i32)
        slots_f = sb("slots_f", [P, E])
        slots_end = sb("slots_end", [P, E])
        base_row = sb("base_row", [P, E])
        pos = sb("pos", [P, K, NT], i32)
        slot_expert = sb("slot_expert", [1, SLOTS], i32)

        nat = region[:, 0:RING * N].rearrange("p (r n) -> p r n", r=RING)
        w1_0 = region[:, 0:E * F].rearrange("p (e f) -> p e f", e=E)
        w2_0 = region[:, E * F:2 * E * F].rearrange("p (e h d) -> p e h d", e=E, h=FH)
        b2_0 = region[:, 2 * E * F:2 * E * F + E * D].rearrange("p (e d) -> p e d", e=E)
        w12_1 = region[:, 0:2 * E * F].rearrange("p (e w f) -> p e w f", e=E, w=2)
        w3_1 = adjT[:, 0:2, :].rearrange("p a n -> p (a n)").rearrange("p (e h d) -> p e h d", e=E, h=FH)
        silu = adjT[:, 2, 0:2 * F].rearrange("p (b f) -> p b f", b=2)
        exact = region[:, 0:N]
        remain = region[:, N:2 * N + 8]
        top8 = region[:, 2 * N + 8:2 * N + 16]

        xnT = gath[:, :, :, :].rearrange("p k r d -> p k (r d)")
        tmpA = hbuf[:, 0:2, :].rearrange("p a f -> p (a f)")
        tmpB = hbuf[:, 2:4, :].rearrange("p a f -> p (a f)")
        tmpC = slot_in[:, :, :].rearrange("p a f -> p (a f)")
        tmpD = slot_out[:, :, :].rearrange("p a f -> p (a f)")
        logits = tmpC[:, 0:NT * E].rearrange("p (t e) -> p t e", t=NT)
        ends = tmpC[0:1, 0:SLOTS * E // 2].rearrange("p (s e) -> p s e", s=SLOTS)
        se_half = tmpC[0:1, SLOTS * E // 2:SLOTS * E // 2 + SLOTS]
        se_f = tmpC[0:1, 424:424 + SLOTS]
        pos_f = tmpC[:, 480:480 + C]
        b1_rows = tmpC[0:E, 0:F]
        iota_i = tmpC[:, F:F + E + SLOTS].bitcast(i32)
        onehot = tmpD[:, 0:E * C // 2].bitcast(bf16).rearrange("p (e k t) -> p e k t", e=E, k=K)
        top = tmpD[:, E * C // 2:E * C // 2 + NT * 8].rearrange("p (t n) -> p t n", t=NT)
        topi = tmpD[:, E * C // 2 + NT * 8:E * C // 2 + NT * 16].rearrange("p (t n) -> p t n", t=NT).bitcast(u32)
        hmid = hbuf[:, 0:2, :]
        hidT = hbuf[:, 2:4, :]
        junkA = wide[:, :, :].rearrange("p a n -> p (a n)").bitcast(bf16)
        junkV = xnT.rearrange("p a n -> p (a n)").bitcast(bf16)

        bank = [ctx.enter_context(nc.psum_tensor(f"bank{n}", [P, 512], f32)) for n in range(8)]

        dispatched = nc.dram_tensor("dispatched", (SLOTS * P, D), f32, kind="Internal").ap()
        expert_out = nc.dram_tensor("expert_out", (SLOTS * P, D), f32, kind="Internal").ap()

        x_in = sem("x_in")
        small_in = sem("small_in")
        nat_in = [sem(f"nat_in{n}") for n in range(RING)]
        weights_in = [sem("weights_in0"), sem("weights_in1")]
        w3_in = sem("w3_in")
        zeroed = sem("zeroed")
        pool_step = sem("pool_step")
        consts = sem("consts")
        dve_step = sem("dve_step")
        b1_turned = sem("b1_turned")
        b1_ready = sem("b1_ready")
        adj_turned = sem("adj_turned")
        adjT_dve = sem("adjT_dve")
        adjT_act = sem("adjT_act")
        deg_ready = sem("deg_ready")
        nnz_ready = sem("nnz_ready")
        xs_ready = sem("xs_ready")
        agg_done = [sem("agg_done0"), sem("agg_done1")]
        agg_out = [sem("agg_out0"), sem("agg_out1")]
        z_done = [sem("z_done0"), sem("z_done1")]
        z_used = [sem("z_used0"), sem("z_used1")]
        elu_min = sem("elu_min")
        elu_exp = sem("elu_exp")
        xn_ready = [sem("xn_ready0"), sem("xn_ready1")]
        xn_turned = [sem("xn_turned0"), sem("xn_turned1")]
        xnT_ready = [sem("xnT_ready0"), sem("xnT_ready1")]
        logits_done = [sem("logits_done0"), sem("logits_done1")]
        gap_ready = [sem("gap_ready0"), sem("gap_ready1")]
        gap_exp = [sem("gap_exp0"), sem("gap_exp1")]
        onehot_ready = [sem("onehot_ready0"), sem("onehot_ready1")]
        ranks_done = [sem("ranks_done0"), sem("ranks_done1")]
        routed = [sem("routed0"), sem("routed1")]
        scattered = [sem("scattered0"), sem("scattered1")]
        squared = sem("squared")
        filtered = sem("filtered")
        row_in = [[sem(f"row_in{l}_{n}") for n in range(RING)] for l in range(2)]
        row_turned = [sem("row_turned0"), sem("row_turned1")]
        rowT_ready = [sem("rowT_ready0"), sem("rowT_ready1")]
        up_done = [sem("up_done0"), sem("up_done1")]
        silu_ready = sem("silu_ready")
        hid_ready = [sem("hid_ready0"), sem("hid_ready1")]
        hid_turned = [sem("hid_turned0"), sem("hid_turned1")]
        hidT_ready = [sem("hidT_ready0"), sem("hidT_ready1")]
        down_done = [sem("down_done0"), sem("down_done1")]
        out_ready = [sem("out_ready0"), sem("out_ready1")]
        row_out = [[sem(f"row_out{l}_{n}") for n in range(RING)] for l in range(2)]
        fetched = [[sem(f"fetched{l}_{n}") for n in range(RING)] for l in range(2)]
        combined = [sem("combined0"), sem("combined1")]
        xn1_ready = sem("xn1_ready")
        xn1_turned = sem("xn1_turned")
        xn1T_ready = sem("xn1T_ready")
        proj_done = sem("proj_done")
        h2_ready = sem("h2_ready")
        feat_done = sem("feat_done")
        feat_ready = sem("feat_ready")
        exact_in = sem("exact_in")
        exact_sq = sem("exact_sq")
        exact_tanh = sem("exact_tanh")
        exact_step = sem("exact_step")
        exact_kept = sem("exact_kept")
        exact_turned = sem("exact_turned")
        exact_used = sem("exact_used")
        stored = sem("stored")

        SMALL = 14
        block = ctx.enter_context(nc.Block())

        def run_slots(engine, step, depth):
            first = RING * (1 - (-depth // RING))
            last = RING * (SLOTS // RING)
            for s in range(first):
                step(s, s, s, s // RING, s % RING)
            with engine.Fori(first // RING, last // RING) as i:
                for h in range(RING):
                    step(i * RING + h, first + h, last - RING + h, i, h)
            for s in range(last, SLOTS + depth):
                step(s, s, s, s // RING, s % RING)

        def live(lo, hi, back):
            return lo - back >= 0 and hi - back < SLOTS

        def rounds(i, h, back):
            return i + (h - back) // RING, (h - back) % RING

        def slot_rows(tensor, s):
            return tensor[bass.ds(s * P, P), :]

        @block.sync
        def _(sp):
            sp.dma_start(xres[:], x.rearrange("(t p) d -> p t d", p=P)).then_inc(x_in, 16)
            for r in range(RING):
                sp.dma_start(nat[:, r, :], adj[r * P:(r + 1) * P, :]).then_inc(nat_in[r], 16)
            with sp.Fori(1, NT // RING) as i:
                for r in range(RING):
                    sp.wait_ge(adj_turned, (i * RING + r - RING + 1) * GT)
                    sp.wait_ge(deg_ready, i * RING + r - RING + 1)
                    sp.wait_ge(nnz_ready, i * RING + r - RING + 1)
                    sp.dma_start(nat[:, r, :], adj[bass.ds((i * RING + r) * P, P), :]).then_inc(nat_in[r], 16)
            sp.wait_ge(consts, 1)
            for s0 in range(0, SLOTS, 16):
                n = min(16, SLOTS - s0)
                sp.dma_start(dispatched[s0 * P:(s0 + n) * P, :].rearrange("(s p) d -> p s d", p=P),
                             ident[:, :].unsqueeze(1).to_broadcast([P, n, D])).then_inc(zeroed, 16)
            sp.wait_ge(adj_turned, NT * GT)
            sp.wait_ge(deg_ready, NT)
            sp.wait_ge(nnz_ready, NT)
            sp.dma_start(w1_0, L0_ffn_w1.rearrange("e d f -> d e f")).then_inc(weights_in[0], 16)
            sp.dma_start(w2_0, L0_ffn_w2.rearrange("e (h p) d -> p e h d", p=P)).then_inc(weights_in[0], 16)
            sp.dma_start(region[:, 2 * E * F:2 * E * F + E * D],
                         L0_ffn_b2.rearrange("e d -> (e d)").partition_broadcast(P)).then_inc(weights_in[0], 16)

            def slots(l):
                def step(s, lo, hi, i, h):
                    if live(lo, hi, 0):
                        if lo >= RING:
                            sp.wait_ge(row_turned[l], s - RING + 1)
                        sp.dma_start(slot_in[:, h, :], slot_rows(dispatched, s)).then_inc(row_in[l][h], 16)
                    if live(lo, hi, 8):
                        sp.wait_ge(out_ready[l], s - 8 + 1)
                        sp.dma_start(slot_rows(expert_out, s - 8), slot_out[:, h, :]).then_inc(row_out[l][h], 16)

                sp.wait_ge(scattered[l], 16 * C)
                run_slots(sp, step, 8)

            slots(0)
            sp.wait_ge(down_done[0], SLOTS)
            sp.wait_ge(out_ready[0], SLOTS)
            fl = sp.value_load(flag[0:1, 0:1], min_val=0, max_val=N)
            with sp.If(fl > 0):
                with sp.Fori(0, NT) as r:
                    sp.wait_ge(exact_used, r + 1)
                    sp.dma_start(exact, adj[bass.ds(r * P, P), :]).then_inc(exact_in, 16)
                sp.wait_ge(exact_used, NT + 1)
            sp.dma_start(w12_1[:, :, 0, :], L1_ffn_w1.rearrange("e d f -> d e f")).then_inc(weights_in[1], 16)
            sp.dma_start(w12_1[:, :, 1, :], L1_ffn_w2.rearrange("e d f -> d e f")).then_inc(weights_in[1], 16)
            sp.wait_ge(agg_done[1], NG)
            sp.dma_start(w3_1, L1_ffn_w3.rearrange("e (h p) d -> p e h d", p=P)).then_inc(w3_in, 16)
            slots(1)
            for g in range(NG):
                sp.wait_ge(combined[1], (g + 1) * GT)
                sp.dma_start(out[g * GW:(g + 1) * GW, :].rearrange("(t p) d -> p t d", p=P),
                             xres[:, g * GT:(g + 1) * GT, :]).then_inc(stored, 16)
            sp.wait_ge(stored, 16 * NG)

        @block.gpsimd
        def _(pool):
            steps = Count(pool, pool_step)
            steps.inc(nc.gpsimd.memset(ident[:], 1.0))
            steps.inc(nc.gpsimd.memset(ones[:], 1.0))
            steps.inc(nc.gpsimd.memset(segment[:], 1.0))
            steps.inc(nc.gpsimd.iota(iota_i[:, 0:E], pattern=[[1, E]], base=0, channel_multiplier=0))
            steps.inc(nc.gpsimd.iota(iota_i[:, E:E + SLOTS], pattern=[[1, SLOTS]], base=0, channel_multiplier=0))
            steps.wait()
            steps.inc(nc.gpsimd.affine_select(out=ident[:], in_=ident[:], compare_op=ALU.is_equal, fill=0.0,
                                              base=0, pattern=[[-1, P]], channel_multiplier=1))
            steps.inc(nc.gpsimd.affine_select(out=before[:], in_=ones[:], compare_op=ALU.is_gt, fill=0.0,
                                              base=0, pattern=[[1, P]], channel_multiplier=-1))
            steps.inc(nc.gpsimd.memset(segment[:, :].rearrange("p (e c) -> p e c", c=C)[:, :, 0:1], 0.0))
            steps.inc(nc.gpsimd.tensor_copy(iota_e[:], iota_i[:, 0:E]))
            steps.inc(nc.gpsimd.tensor_copy(iota_s[:], iota_i[0:1, E:E + SLOTS]))
            steps.wait()
            nc.gpsimd.memset(flag[:], 0).then_inc(consts, 1)

            for l in range(2):
                pool.wait_ge(routed[l], 1)
                if l == 0:
                    pool.wait_ge(zeroed, 16 * -(-SLOTS // 16))
                for k in range(K):
                    for t in range(NT):
                        nc.gpsimd.indirect_dma_start(
                            out=dispatched, out_offset=bass.IndirectOffsetOnAxis(ap=pos[:, k, t:t + 1], axis=0),
                            in_=xn[:, t, :], in_offset=None).then_inc(scattered[l], 16)
                for h in range(RING):
                    pool.wait_ge(row_out[l][h], 16 * len(range(h, SLOTS, RING)))
                for t in range(NT):
                    if t >= RING:
                        pool.wait_ge(combined[l], t - RING + 1)
                    for k in range(K):
                        nc.gpsimd.indirect_dma_start(
                            out=gath[:, k, t % RING, :], out_offset=None, in_=expert_out,
                            in_offset=bass.IndirectOffsetOnAxis(ap=pos[:, k, t:t + 1], axis=0),
                        ).then_inc(fetched[l][t % RING], 16)

        @block.scalar
        def _(act):
            for dst, src in [
                (gnn_w[:], L0_gnn_w), (proj_w[:], L1_gnn_W_proj), (gcn_w[:], L1_gnn_W_gcn),
                (proj_b[:], L1_gnn_b_proj.unsqueeze(1)), (gcn_b[:], L1_gnn_b_gcn.unsqueeze(1)),
                (gate_w[0][:], L0_ffn_gate_w), (gate_w[1][:], L1_ffn_gate_w),
                (gate_b[0][:], L0_ffn_gate_b.partition_broadcast(P)),
                (gate_b[1][:], L1_ffn_gate_b.partition_broadcast(P)),
                (gamma[:], L0_ffn_gamma.partition_broadcast(P)), (beta[:], L0_ffn_beta.partition_broadcast(P)),
                (b1_rows, L0_ffn_b1),
            ]:
                act.dma_start(dst, src).then_inc(small_in, 16)

            with act.Fori(0, NT // RING) as i:
                for r in range(RING):
                    act.wait_ge(nat_in[r], (i + 1) * 16)
                    nc.scalar.activation(junkA, nat[:, r, :], ACT.Copy,
                                         accum_out=deg[:, bass.ds(i * RING + r, 1)]).then_inc(deg_ready, 1)
                    for q in (2, 3):
                        act.wait_ge(adj_turned, (i * RING + r) * GT + q + 1)
                        nc.scalar.copy(adjT[:, q * GT:(q + 1) * GT, bass.ds((i * RING + r) * P, P)],
                                       bank[4 + q][:, :].rearrange("p (a b) -> p a b", a=GT)).then_inc(adjT_act, 1)
                    act.wait_ge(deg_ready, i * RING + r + 1)

            def after_aggregation(l):
                for s in range(NG + 1):
                    if s < NG:
                        act.wait_ge(agg_done[l], s + 1)
                        if s >= 2:
                            act.wait_ge(z_done[l], s - 1)
                        if l == 0:
                            nc.scalar.copy(wide[:, s % 2, :], bank[s][:]).then_inc(agg_out[l], 1)
                        else:
                            nc.scalar.activation(wide[:, s % 2, :], bank[s][:], ACT.Relu,
                                                 bias=gcn_b[:, 0:1]).then_inc(agg_out[l], 1)
                    if 1 <= s <= NG and l == 0:
                        act.wait_ge(elu_min, s)
                        nc.scalar.activation(tmpB, tmpB, ACT.Exp).then_inc(elu_exp, 1)
                for g in range(NG):
                    act.wait_ge(xn_turned[l], g + 1)
                    if g >= 2:
                        act.wait_ge(logits_done[l], g - 1)
                    nc.scalar.copy(xnT[:, g % 2, :], bank[6 + g % 2][:]).then_inc(xnT_ready[l], 1)
                act.wait_ge(gap_ready[l], 1)
                nc.scalar.activation(wexp[:], wexp[:], ACT.Exp).then_inc(gap_exp[l], 1)

            after_aggregation(0)
            with act.Fori(0, NT) as t:
                act.wait_ge(squared, t + 1)
                nc.scalar.activation(adjT[:, bass.ds(t, 1), :], adjT[:, bass.ds(t, 1), :],
                                     ACT.Tanh).then_inc(filtered, 1)

            def step0(s, lo, hi, i, h):
                if live(lo, hi, 2):
                    e = act.value_load(slot_expert[0:1, bass.ds(s - 2, 1)], min_val=0, max_val=E - 1)
                    act.wait_ge(hid_turned[0], s - 2 + 1)
                    pt = bank[4 + (h - 2) % 2]
                    for f in range(FH):
                        last = nc.scalar.activation(hidT[:, (h - 2) % 2, f * P:(f + 1) * P], pt[:, f * P:(f + 1) * P],
                                                    ACT.Relu, bias=b1T[:, f, bass.ds(e, 1)])
                    last.then_inc(hidT_ready[0], 1)

            act.wait_ge(routed[0], 1)
            act.wait_ge(b1_ready, 1)
            run_slots(act, step0, 2)

            for g in range(NG):
                act.wait_ge(xn1_turned, g + 1)
                nc.scalar.copy(wide[:, 0, :], bank[4][:]).then_inc(xn1T_ready, 1)
                act.wait_ge(proj_done, g + 1)
                nc.scalar.activation(wide[:, 1, :], bank[5][:], ACT.Tanh, bias=proj_b[:, 0:1]).then_inc(h2_ready, 1)
                act.wait_ge(feat_done, g + 1)
                nc.scalar.copy(xn[:, g * GT:(g + 1) * GT, :],
                               bank[6][:, :].rearrange("p (a b) -> p a b", a=GT)).then_inc(feat_ready, 1)

            fl = act.value_load(flag[0:1, 0:1], min_val=0, max_val=N)
            with act.If(fl > 0):
                with act.Fori(0, NT) as r:
                    act.wait_ge(exact_sq, r + 1)
                    nc.scalar.activation(exact, exact, ACT.Tanh).then_inc(exact_tanh, 1)

            after_aggregation(1)

            def step1(s, lo, hi, i, h):
                if live(lo, hi, 3):
                    ri, rh = rounds(i, h, 3)
                    act.wait_ge(down_done[1], s - 3 + 1)
                    if lo - 3 >= RING:
                        act.wait_ge(row_out[1][rh], 16 * ri)
                    nc.scalar.copy(slot_out[:, rh, :], bank[6 + (h - 3) % 2][:, 0:D]).then_inc(out_ready[1], 1)
                if live(lo, hi, 1):
                    b = (h - 1) % 2
                    act.wait_ge(up_done[1], s - 1 + 1)
                    if lo - 1 >= 2:
                        act.wait_ge(hid_ready[1], s - 1 - 1)
                    nc.scalar.activation(silu[:, b, :], bank[2 + b][:, 0:F], ACT.Silu).then_inc(silu_ready, 1)

            run_slots(act, step1, 3)

        @block.vector
        def _(dve):
            V = nc.vector
            steps = Count(dve, dve_step)

            def rsqrt(y, v, add):
                steps.inc(V.tensor_scalar(root_v[:], v, add, None, ALU.add))
                steps.wait()
                steps.inc(V.tensor_scalar(y.bitcast(i32), root_v[:, :].bitcast(i32), -0.5, float(0x5F3759DF),
                                          ALU.mult, ALU.add))
                for _ in range(3):
                    steps.wait()
                    steps.inc(V.tensor_tensor(root_t[:], y, y, ALU.mult))
                    steps.wait()
                    steps.inc(V.scalar_tensor_tensor(out=root_t[:], in0=root_t[:], scalar=-0.5, in1=root_v[:],
                                                     op0=ALU.mult, op1=ALU.mult))
                    steps.wait()
                    steps.inc(V.scalar_tensor_tensor(out=y, in0=root_t[:], scalar=1.5, in1=y,
                                                     op0=ALU.add, op1=ALU.mult))
                steps.wait()

            def layer_stats(src, t0, n):
                for t in range(t0, t0 + n):
                    steps.inc(V.bn_stats(stats[:, t % GT, :], src[:, t, :]))
                steps.wait()
                for t in range(t0, t0 + n):
                    steps.inc(V.bn_aggr(mv[:, t, :], stats[:, t % GT, :]))
                steps.wait()
                rsqrt(rstd[:, t0:t0 + n], mv[:, t0:t0 + n, 1], EPS)

            def layer_shift(t0, n):
                steps.inc(V.scalar_tensor_tensor(out=shift[:, t0:t0 + n], in0=mv[:, t0:t0 + n, 0], scalar=-1.0,
                                                 in1=rstd[:, t0:t0 + n], op0=ALU.mult, op1=ALU.mult))
                steps.wait()

            def apply(dst, src, t0, n, signal=None):
                for t in range(t0, t0 + n):
                    last = V.tensor_scalar(dst[:, t, :], src[:, t, :], rstd[:, t:t + 1], shift[:, t:t + 1],
                                           ALU.mult, ALU.add)
                    if signal is None:
                        steps.inc(last)
                    elif t == t0 + n - 1:
                        last.then_inc(signal, 1)
                if signal is None:
                    steps.wait()

            dve.wait_ge(x_in, 16)
            for g in range(NG):
                layer_stats(xres, g * GT, GT)

            for g in range(NG):
                for r in range(RING):
                    t = g * RING + r
                    dve.wait_ge(nat_in[r], (g + 1) * 16)
                    V.tensor_scalar(junkV, nat[:, r, :], 0.0, 0.0, ALU.is_gt, ALU.add,
                                    accum_out=nnz[:, t:t + 1]).then_inc(nnz_ready, 1)
                    for q in (0, 1):
                        dve.wait_ge(adj_turned, t * GT + q + 1)
                        V.tensor_copy(adjT[:, q * GT:(q + 1) * GT, t * P:(t + 1) * P],
                                      bank[4 + q][:, :].rearrange("p (a b) -> p a b", a=GT)).then_inc(adjT_dve, 1)
                    dve.wait_ge(nnz_ready, t + 1)
                t0 = g * GT
                dve.wait_ge(deg_ready, t0 + GT)
                rsqrt(dis[:, t0:t0 + GT], deg[:, t0:t0 + GT], 1.0)
                steps.inc(V.tensor_tensor(rstd[:, t0:t0 + GT], rstd[:, t0:t0 + GT], dis[:, t0:t0 + GT], ALU.mult))
                steps.wait()
                layer_shift(t0, GT)
                apply(xn, xres, t0, GT, xs_ready)

            dve.wait_ge(nnz_ready, NT)
            steps.inc(V.tensor_scalar(over[:], nnz[:], float(TOP), None, ALU.is_gt))
            steps.wait()
            steps.inc(V.tensor_reduce(over_any[:], over[:], AX, ALU.max))
            dve.wait_ge(small_in, 16 * 12)
            dve.wait_ge(b1_turned, 1)
            V.tensor_copy(b1T[:, :, :], bank[4][:, 0:FH * E].rearrange("p (f e) -> p f e", f=FH)).then_inc(b1_ready, 1)

            def graph_to_residual(l, g):
                t0 = g * GT
                xg = xres[:, t0:t0 + GT, :]
                z = bank[4 + g % 2][:, :].rearrange("p (t d) -> p t d", t=GT)
                A3 = tmpA.rearrange("p (t d) -> p t d", t=GT)
                dve.wait_ge(z_done[l], g + 1)
                if l == 1:
                    V.tensor_tensor(xg, z, xg, ALU.add).then_inc(z_used[l], 1)
                    dve.wait_ge(z_used[l], g + 1)
                    return
                V.tensor_tensor(A3, z, dis[:, t0:t0 + GT].unsqueeze(2).to_broadcast([P, GT, D]),
                                ALU.mult).then_inc(z_used[l], 1)
                dve.wait_ge(z_used[l], g + 1)
                V.tensor_scalar(tmpB, tmpA, 0.0, None, ALU.min).then_inc(elu_min, 1)
                dve.wait_ge(elu_exp, g + 1)
                steps.inc(V.scalar_tensor_tensor(out=tmpA, in0=tmpA, scalar=0.0, in1=tmpB, op0=ALU.max, op1=ALU.add))
                steps.wait()
                steps.inc(V.scalar_tensor_tensor(out=xg, in0=A3, scalar=-1.0, in1=xg, op0=ALU.add, op1=ALU.add))
                steps.wait()

            def gate_group(l, g):
                t0 = g * GT
                lg = logits[:, t0:t0 + GT, :]
                dve.wait_ge(logits_done[l], g + 1)
                steps.inc(V.tensor_tensor(lg, bank[g][:, 0:GT * E].rearrange("p (t e) -> p t e", t=GT),
                                          gate_b[l][:, :].unsqueeze(1).to_broadcast([P, GT, E]), ALU.add))
                steps.wait()
                for t in range(GT):
                    steps.inc(V.max(out=top[:, t0 + t, :], in_=lg[:, t, :]))
                steps.wait()
                for t in range(GT):
                    steps.inc(V.max_index(out=topi[:, t0 + t, :], in_max=top[:, t0 + t, :], in_values=lg[:, t, :]))

            def after_aggregation(l):
                for g in range(NG):
                    graph_to_residual(l, g)
                    layer_stats(xres, g * GT, GT)
                    layer_shift(g * GT, GT)
                dve.wait_ge(agg_done[l], NG)
                for s in range(NG + 1):
                    if s < NG:
                        apply(xn, xres, s * GT, GT, xn_ready[l])
                    if s >= 1:
                        gate_group(l, s - 1)
                steps.wait()

            def route(l):
                V.tensor_tensor(wexp[:], top[:, :, 1], top[:, :, 0], ALU.subtract).then_inc(gap_ready[l], 1)
                steps.inc(V.tensor_copy(chosen[:, :, :], topi[:, :, 0:K].rearrange("p t k -> p k t")))
                steps.wait()
                for k in range(K):
                    V.tensor_tensor(onehot[:, :, k, :], iota_e[:, :].unsqueeze(2).to_broadcast([P, E, NT]),
                                    chosen[:, k, :].unsqueeze(1).to_broadcast([P, E, NT]),
                                    ALU.is_equal).then_inc(onehot_ready[l], 1)
                dve.wait_ge(onehot_ready[l], K)
                dve.wait_ge(gap_exp[l], 1)
                steps.inc(V.tensor_scalar(wsum[:], wexp[:], 1.0, None, ALU.add))
                steps.wait()
                steps.inc(V.reciprocal(wk[:, 0, :], wsum[:]))
                steps.wait()
                steps.inc(V.tensor_tensor(wk[:, 1, :], wk[:, 0, :], wexp[:], ALU.mult))
                dve.wait_ge(ranks_done[l], 1)
                steps.inc(V.tensor_tensor_scan(tmpA, segment[:], bank[2][:], 0.0, ALU.mult, ALU.add))
                steps.wait()
                steps.inc(V.tensor_copy(count_i[:], tmpA.rearrange("p (e c) -> p e c", c=C)[:, :, C - 1]))
                steps.inc(V.tensor_tensor(tmpB, tmpA, bank[2][:], ALU.subtract))
                steps.wait()
                steps.inc(V.tensor_scalar(count_i[:], count_i[:], P - 1, None, ALU.add))
                steps.inc(V.tensor_tensor(tmpA, tmpB, bank[1][:], ALU.add))
                steps.wait()
                steps.inc(V.tensor_scalar(count_i[:], count_i[:], P.bit_length() - 1, None, ALU.arith_shift_right))
                steps.wait()
                steps.inc(V.tensor_copy(slots_f[:], count_i[:]))
                steps.wait()
                steps.inc(V.tensor_tensor_scan(slots_end[:], ones[:, 0:E], slots_f[:], 0.0, ALU.mult, ALU.add))
                steps.wait()
                steps.inc(V.tensor_tensor(base_row[:], slots_end[:], slots_f[:], ALU.subtract))
                steps.wait()
                steps.inc(V.tensor_scalar(base_row[:], base_row[:], float(P), None, ALU.mult))
                steps.wait()
                A3, B3 = (a.rearrange("p (e c) -> p e c", c=C) for a in (tmpA, tmpB))
                steps.inc(V.tensor_tensor(B3, A3, base_row[:, :].unsqueeze(2).to_broadcast([P, E, C]), ALU.add))
                steps.wait()
                steps.inc(V.tensor_tensor(tmpA, tmpB, onehot.rearrange("p e k t -> p (e k t)"), ALU.mult))
                steps.wait()
                steps.inc(V.tensor_reduce(pos_f,
                                          tmpA.rearrange("p (e c) -> p c e", c=C), AX, ALU.add))
                steps.wait()
                steps.inc(V.tensor_copy(pos[:, :, :].rearrange("p k t -> p (k t)"), pos_f))
                for half in range(2):
                    steps.wait()
                    steps.inc(V.tensor_tensor(
                        ends, slots_end[0:1, half * E // 2:(half + 1) * E // 2].unsqueeze(1).to_broadcast([1, SLOTS, E // 2]),
                        iota_s[0:1, :].unsqueeze(2).to_broadcast([1, SLOTS, E // 2]), ALU.is_le))
                    steps.wait()
                    steps.inc(V.tensor_reduce((se_half if half else se_f), ends, AX, ALU.add))
                steps.wait()
                steps.inc(V.tensor_tensor(se_f[:], se_f[:], se_half, ALU.add))
                steps.wait()
                steps.inc(V.tensor_scalar(se_f[:], se_f[:], float(E - 1), None, ALU.min))
                steps.wait()
                V.tensor_copy(slot_expert[:], se_f[:]).then_inc(routed[l], 1)
                dve.wait_ge(routed[l], 1)

            after_aggregation(0)
            route(0)
            steps.inc(V.tensor_copy(flag[0:1, 0:1], bank[4][0:1, 0:1]))
            with dve.Fori(0, NT) as t:
                a = adjT[:, bass.ds(t, 1), :]
                V.scalar_tensor_tensor(out=a, in0=a, scalar=0.0, in1=a, op0=ALU.max, op1=ALU.mult).then_inc(squared, 1)

            def step0(s, lo, hi, i, h):
                if live(lo, hi, 3):
                    ri, rh = rounds(i, h, 3)
                    e = dve.value_load(slot_expert[0:1, bass.ds(s - 3, 1)], min_val=0, max_val=E - 1)
                    dve.wait_ge(down_done[0], s - 3 + 1)
                    if lo - 3 >= RING:
                        dve.wait_ge(row_out[0][rh], 16 * ri)
                    V.tensor_tensor(slot_out[:, rh, :], bank[6 + (h - 3) % 2][:, 0:D], b2_0[:, bass.ds(e, 1), :],
                                    ALU.add).then_inc(out_ready[0], 1)
                if live(lo, hi, 1):
                    b = (h - 1) % 2
                    dve.wait_ge(up_done[0], s - 1 + 1)
                    V.tensor_copy(hmid[:, b, :], bank[2 + b][:, 0:F]).then_inc(hid_ready[0], 1)
                if live(lo, hi, 0):
                    dve.wait_ge(row_turned[0], s + 1)
                    V.tensor_copy(slotT[:, h % 2, :], bank[h % 2][:, 0:P]).then_inc(rowT_ready[0], 1)

            dve.wait_ge(weights_in[0], 16 * 3)
            run_slots(dve, step0, 3)

            G3 = [a.rearrange("p (t d) -> p t d", t=GT) for a in (tmpA, tmpB)]
            for g in range(NG):
                t0 = g * GT
                for t in range(t0, t0 + GT):
                    r = t % RING
                    dve.wait_ge(fetched[0][r], 16 * K * (t // RING + 1))
                    steps.inc(V.scalar_tensor_tensor(out=xn[:, t, :], in0=gath[:, 0, r, :], scalar=wk[:, 0, t:t + 1],
                                                     in1=xn[:, t, :], op0=ALU.mult, op1=ALU.add))
                    steps.wait()
                    V.scalar_tensor_tensor(out=xn[:, t, :], in0=gath[:, 1, r, :], scalar=wk[:, 1, t:t + 1],
                                           in1=xn[:, t, :], op0=ALU.mult, op1=ALU.add).then_inc(combined[0], 1)
                dve.wait_ge(combined[0], t0 + GT)
                layer_stats(xn, t0, GT)
                layer_shift(t0, GT)
                apply(xn, xn, t0, GT)
                xg, yg = xres[:, t0:t0 + GT, :], xn[:, t0:t0 + GT, :]
                steps.inc(V.tensor_tensor(G3[0], yg, gamma[:, :].unsqueeze(1).to_broadcast([P, GT, D]), ALU.mult))
                steps.wait()
                steps.inc(V.tensor_tensor(G3[1], G3[0], beta[:, :].unsqueeze(1).to_broadcast([P, GT, D]), ALU.add))
                steps.wait()
                steps.inc(V.tensor_tensor(xg, G3[1], xg, ALU.add))
                steps.wait()
                layer_stats(xres, t0, GT)
                layer_shift(t0, GT)
                apply(xn, xres, t0, GT, xn1_ready)

            fl = dve.value_load(flag[0:1, 0:1], min_val=0, max_val=N)
            with dve.If(fl > 0):
                dve.wait_ge(down_done[0], SLOTS)
                dve.wait_ge(filtered, NT)
                rounds_full, rest = TOP // 8, TOP % 8
                V.memset(over[:, 0:1], 0.0).then_inc(exact_used, 1)
                with dve.Fori(0, NT) as r:
                    per = 3 + 2 * rounds_full + 3
                    k = [0]

                    def chained(ins):
                        ins.then_inc(exact_step, 1)
                        k[0] += 1
                        dve.wait_ge(exact_step, r * per + k[0])
                        V.memset(over[:, 1:2], 0.0)

                    dve.wait_ge(exact_in, (r + 1) * 16)
                    V.scalar_tensor_tensor(out=exact, in0=exact, scalar=0.0, in1=exact, op0=ALU.max,
                                           op1=ALU.mult).then_inc(exact_sq, 1)
                    dve.wait_ge(exact_tanh, r + 1)
                    chained(V.tensor_copy(remain[:, 0:N], exact))
                    chained(V.memset(remain[:, N:N + 8], -1.0))
                    for _ in range(rounds_full):
                        chained(V.max(out=top8, in_=remain))
                        chained(V.match_replace(out=remain, in_to_replace=top8, in_values=remain, imm_value=0.0))
                    chained(V.max(out=top8, in_=remain))
                    chained(V.memset(top8[:, rest:8], -1.0))
                    chained(V.match_replace(out=remain, in_to_replace=top8, in_values=remain, imm_value=0.0))
                    chained(V.tensor_tensor(remain[:, 0:N], exact, remain[:, 0:N], ALU.subtract))
                    assert k[0] == per
                    for q in range(GT):
                        dve.wait_ge(exact_turned, r * GT + q + 1)
                        last = V.tensor_copy(adjT[:, q * GT:(q + 1) * GT, bass.ds(r * P, P)],
                                             bank[4 + q % 2][:, :].rearrange("p (a b) -> p a b", a=GT))
                        last.then_inc(exact_kept, 1)
                    dve.wait_ge(exact_kept, (r + 1) * GT)
                    V.memset(over[:, 0:1], 0.0).then_inc(exact_used, 1)

            after_aggregation(1)
            route(1)

            def step1(s, lo, hi, i, h):
                if live(lo, hi, 2):
                    b = (h - 2) % 2
                    dve.wait_ge(hid_turned[1], s - 2 + 1)
                    V.tensor_copy(hidT[:, b, :], bank[4 + b][:, 0:F]).then_inc(hidT_ready[1], 1)
                if live(lo, hi, 1):
                    b = (h - 1) % 2
                    dve.wait_ge(silu_ready, s - 1 + 1)
                    V.tensor_tensor(hmid[:, b, :], silu[:, b, :], bank[2 + b][:, F:2 * F],
                                    ALU.mult).then_inc(hid_ready[1], 1)
                if live(lo, hi, 0):
                    dve.wait_ge(row_turned[1], s + 1)
                    V.tensor_copy(slotT[:, h % 2, :], bank[h % 2][:, 0:P]).then_inc(rowT_ready[1], 1)

            run_slots(dve, step1, 2)

            for t in range(NT):
                r = t % RING
                dve.wait_ge(fetched[1][r], 16 * K * (t // RING + 1))
                steps.inc(V.scalar_tensor_tensor(out=xres[:, t, :], in0=gath[:, 0, r, :], scalar=wk[:, 0, t:t + 1],
                                                 in1=xres[:, t, :], op0=ALU.mult, op1=ALU.add))
                steps.wait()
                V.scalar_tensor_tensor(out=xres[:, t, :], in0=gath[:, 1, r, :], scalar=wk[:, 1, t:t + 1],
                                       in1=xres[:, t, :], op0=ALU.mult, op1=ALU.add).then_inc(combined[1], 1)

        @block.tensor
        def _(pe):
            T = nc.tensor
            pe.wait_ge(consts, 1)

            def aggregate(g, tiles, first, last):
                for j in tiles:
                    ins = T.matmul(bank[g][:], xn[:, j, :], adjT[:, j, g * GW:(g + 1) * GW],
                                   start=(j == first), stop=(j == last))
                return ins

            def adj_rows(g):
                for r in range(RING):
                    t = g * RING + r
                    pe.wait_ge(nat_in[r], (g + 1) * 16)
                    for q in range(GT):
                        if t >= 1:
                            pe.wait_ge(adjT_dve if q < 2 else adjT_act, 2 * (t - 1) + q % 2 + 1)
                        for b in range(GT):
                            last = T.transpose(bank[4 + q][:, b * P:(b + 1) * P],
                                               nat[:, r, (q * GT + b) * P:(q * GT + b + 1) * P], ident[:])
                        last.then_inc(adj_turned, 1)

            for g in range(NG):
                adj_rows(g)
                pe.wait_ge(adjT_dve, 2 * (g + 1) * RING)
                pe.wait_ge(adjT_act, 2 * (g + 1) * RING)
                pe.wait_ge(xs_ready, g + 1)
                if g < NG - 1:
                    for i in range(g + 1):
                        aggregate(i, range(0 if i == g else g * GT, (g + 1) * GT), 0, NT)

            def finish_aggregation(l, g):
                if l == 0:
                    tiles = range(0 if g == NG - 1 else NT - GT, NT)
                    if g == NG - 1:
                        aggregate(g, range(0, GT), 0, NT)
                        tiles = range(GT, NT)
                    for b in range(GT):
                        T.matmul(bank[g][:, b * P:(b + 1) * P], xn[:, g * GT + b, :], ident[:], start=False, stop=False)
                    aggregate(g, tiles, -1, NT - 1).then_inc(agg_done[0], 1)
                else:
                    aggregate(g, range(NT), 0, NT - 1).then_inc(agg_done[1], 1)

            def to_token_major(l, g):
                pe.wait_ge(agg_out[l], g + 1)
                if g >= 2:
                    pe.wait_ge(z_used[l], g - 1)
                for b in range(GT):
                    o, a = bank[4 + g % 2][:, b * P:(b + 1) * P], wide[:, g % 2, b * P:(b + 1) * P]
                    last = T.matmul(o, a, gnn_w[:], start=True, stop=True) if l == 0 else T.transpose(o, a, ident[:])
                last.then_inc(z_done[l], 1)

            def gate_logits(l, g):
                pe.wait_ge(xn_ready[l], g + 1)
                if g >= 2:
                    pe.wait_ge(xnT_ready[l], g - 1)
                for b in range(GT):
                    last = T.transpose(bank[6 + g % 2][:, b * P:(b + 1) * P], xn[:, g * GT + b, :], ident[:])
                last.then_inc(xn_turned[l], 1)
                pe.wait_ge(xnT_ready[l], g + 1)
                for b in range(GT):
                    last = T.matmul(bank[g][:, b * E:(b + 1) * E], xnT[:, g % 2, b * P:(b + 1) * P], gate_w[l][:],
                                    start=True, stop=True)
                last.then_inc(logits_done[l], 1)

            def graph_layer_end(l):
                for s in range(NG + 1):
                    if s < NG:
                        finish_aggregation(l, s)
                        if s == 0 and l == 0:
                            pe.wait_ge(small_in, 16 * 12)
                            for f in range(FH):
                                last = T.transpose(bank[4][:, f * E:(f + 1) * E], b1_rows[:, f * P:(f + 1) * P],
                                                   ident[0:E, 0:E])
                            last.then_inc(b1_turned, 1)
                            pe.wait_ge(b1_ready, 1)
                    if s >= 1:
                        to_token_major(l, s - 1)
                for g in range(NG):
                    gate_logits(l, g)
                pe.wait_ge(onehot_ready[l], K)
                T.matmul(bank[1][:], before[:], onehot.rearrange("p e k t -> p (e k t)"),
                         start=True, stop=True)
                if l == 0:
                    T.matmul(bank[4][:, 0:1], ones[:], over_any[:], start=True, stop=True)
                T.matmul(bank[2][:], ones[:], onehot.rearrange("p e k t -> p (e k t)"),
                         start=True, stop=True).then_inc(ranks_done[l], 1)

            def slots(l):
                w_up = w1_0 if l == 0 else w12_1.rearrange("p e w f -> p e (w f)")
                w_down = w2_0 if l == 0 else w3_1
                up = F if l == 0 else 2 * F

                def step(s, lo, hi, i, h):
                    if live(lo, hi, 3):
                        b = (h - 3) % 2
                        e = pe.value_load(slot_expert[0:1, bass.ds(s - 3, 1)], min_val=0, max_val=E - 1)
                        pe.wait_ge(hidT_ready[l], s - 3 + 1)
                        if lo - 3 >= 2:
                            pe.wait_ge(out_ready[l], s - 3 - 1)
                        for f in range(FH):
                            last = T.matmul(bank[6 + b][:, 0:D], hidT[:, b, f * P:(f + 1) * P],
                                            w_down[:, bass.ds(e, 1), f, :], start=(f == 0), stop=(f == FH - 1))
                        last.then_inc(down_done[l], 1)
                    if live(lo, hi, 2):
                        b = (h - 2) % 2
                        pe.wait_ge(hid_ready[l], s - 2 + 1)
                        if lo - 2 >= 2:
                            pe.wait_ge(hidT_ready[l], s - 2 - 1)
                        for f in range(FH):
                            last = T.transpose(bank[4 + b][:, f * P:(f + 1) * P], hmid[:, b, f * P:(f + 1) * P], ident[:])
                        last.then_inc(hid_turned[l], 1)
                    if live(lo, hi, 1):
                        b = (h - 1) % 2
                        e = pe.value_load(slot_expert[0:1, bass.ds(s - 1, 1)], min_val=0, max_val=E - 1)
                        pe.wait_ge(rowT_ready[l], s - 1 + 1)
                        if lo - 1 >= 2:
                            pe.wait_ge(hid_ready[l], s - 1 - 1)
                        T.matmul(bank[2 + b][:, 0:up], slotT[:, b, :], w_up[:, bass.ds(e, 1), :],
                                 start=True, stop=True).then_inc(up_done[l], 1)
                    if live(lo, hi, 0):
                        pe.wait_ge(row_in[l][h], 16 * (i + 1))
                        if lo >= 2:
                            pe.wait_ge(rowT_ready[l], s - 1)
                        T.transpose(bank[h % 2][:, 0:P], slot_in[:, h, :], ident[:]).then_inc(row_turned[l], 1)

                pe.wait_ge(routed[l], 1)
                if l == 0:
                    pe.wait_ge(weights_in[0], 16 * 3)
                else:
                    pe.wait_ge(weights_in[1], 16 * 2)
                    pe.wait_ge(w3_in, 16)
                run_slots(pe, step, 3)

            graph_layer_end(0)
            slots(0)

            for g in range(NG):
                pe.wait_ge(xn1_ready, g + 1)
                for b in range(GT):
                    last = T.transpose(bank[4][:, b * P:(b + 1) * P], xn[:, g * GT + b, :], ident[:])
                last.then_inc(xn1_turned, 1)
                pe.wait_ge(xn1T_ready, g + 1)
                T.matmul(bank[5][:], proj_w[:], wide[:, 0, :], start=True, stop=True).then_inc(proj_done, 1)
                pe.wait_ge(h2_ready, g + 1)
                if g >= 1:
                    pe.wait_ge(feat_ready, g)
                for b in range(GT):
                    last = T.matmul(bank[6][:, b * P:(b + 1) * P], wide[:, 1, b * P:(b + 1) * P], gcn_w[:],
                                    start=True, stop=True)
                last.then_inc(feat_done, 1)
            pe.wait_ge(feat_ready, NG)
            pe.wait_ge(filtered, NT)
            fl = pe.value_load(flag[0:1, 0:1], min_val=0, max_val=N)
            with pe.If(fl > 0):
                with pe.Fori(0, NT) as r:
                    pe.wait_ge(exact_step, (r + 1) * (3 + 2 * (TOP // 8) + 3))
                    for q in range(GT):
                        if q >= 2:
                            pe.wait_ge(exact_kept, r * GT + q - 1)
                        for b in range(GT):
                            last = T.transpose(bank[4 + q % 2][:, b * P:(b + 1) * P],
                                               remain[:, (q * GT + b) * P:(q * GT + b + 1) * P], ident[:])
                        last.then_inc(exact_turned, 1)
                    pe.wait_ge(exact_kept, (r + 1) * GT)

            graph_layer_end(1)
            slots(1)


_INS = ['x', 'adj', 'L0_gnn_w', 'L0_ffn_gate_w', 'L0_ffn_gate_b', 'L0_ffn_w1', 'L0_ffn_b1', 'L0_ffn_w2', 'L0_ffn_b2',
        'L0_ffn_gamma', 'L0_ffn_beta', 'L1_gnn_W_proj', 'L1_gnn_b_proj', 'L1_gnn_W_gcn', 'L1_gnn_b_gcn',
        'L1_ffn_gate_w', 'L1_ffn_gate_b', 'L1_ffn_w1', 'L1_ffn_w2', 'L1_ffn_w3']
_OUTS = [((2048, 128), 'float32')]


def kernel(**inputs):
    import numpy as _np
    import concourse.bacc as _bacc
    from concourse import mybir as _mybir
    from concourse.bass_utils import run_bass_kernel_spmd as _run

    nc = _bacc.Bacc("TRN2", target_bir_lowering=False, num_devices=1)
    arrays, args = {}, []
    for name in _INS:
        a = _np.ascontiguousarray(inputs[name])
        arrays[f"in_{name}_dram"] = a
        args.append(nc.dram_tensor(f"in_{name}_dram", a.shape, _mybir.dt.from_np(a.dtype), kind="ExternalInput").ap())
    for i, (shape, dtype) in enumerate(_OUTS):
        dt = _mybir.dt.from_np(_np.dtype(dtype))
        args.append(nc.dram_tensor(f"out_{i}_dram", shape, dt, kind="ExternalOutput").ap())
    gnn_moe_gnn_moe_kernel(nc, *args)
    r = _run(nc, [arrays], core_ids=[0])
    return r.results[0]["out_0_dram"]
```

```python
import concourse.bass as bass
from concourse import mybir
from contextlib import ExitStack


class Count:

    def __init__(self, engine, sem):
        self.engine, self.sem, self.n = engine, sem, 0

    def inc(self, instruction):
        instruction.then_inc(self.sem, 1)
        self.n += 1

    def wait(self):
        self.engine.wait_ge(self.sem, self.n)


def gnn_moe_gnn_moe_kernel(
    nc: bass.Bass,
    x: bass.AP,
    adj: bass.AP,
    L0_gnn_w: bass.AP,
    L0_ffn_gate_w: bass.AP,
    L0_ffn_gate_b: bass.AP,
    L0_ffn_w1: bass.AP,
    L0_ffn_b1: bass.AP,
    L0_ffn_w2: bass.AP,
    L0_ffn_b2: bass.AP,
    L0_ffn_gamma: bass.AP,
    L0_ffn_beta: bass.AP,
    L1_gnn_W_proj: bass.AP,
    L1_gnn_b_proj: bass.AP,
    L1_gnn_W_gcn: bass.AP,
    L1_gnn_b_gcn: bass.AP,
    L1_ffn_gate_w: bass.AP,
    L1_ffn_gate_b: bass.AP,
    L1_ffn_w1: bass.AP,
    L1_ffn_w2: bass.AP,
    L1_ffn_w3: bass.AP,
    out: bass.AP,
):
    f32, bf16 = mybir.dt.float32, mybir.dt.bfloat16
    i32, u32 = mybir.dt.int32, mybir.dt.uint32
    ALU = mybir.AluOpType
    ACT = mybir.ActivationFunctionType
    ENG = mybir.EngineType
    AX = mybir.AxisListType.X

    P = 128
    N, D = x.shape
    E, _, F = L0_ffn_w1.shape
    NT = N // P
    GT = 4
    NG = NT // GT
    GW = GT * P
    K = 2
    TOP = 350
    EPS = 1e-5
    C = K * GT
    RUN = N + P
    SLOTS = (K * N + E * (P - 1)) // P
    RING = 4
    FH = F // P
    ROW = D + 2
    NOBODY = float(2 ** 20)
    LEAD = RING

    ctx = ExitStack()
    with ctx:
        def sb(name, shape, dt=f32):
            return ctx.enter_context(nc.sbuf_tensor(name, shape, dt))

        def sem(name):
            return ctx.enter_context(nc.semaphore(name))

        slot_expert = sb("slot_expert", [1, 64], i32)
        slot_row = sb("slot_row", [1, 64], i32)
        run_end = sb("run_end", [1, E], i32)
        adjT = sb("adjT", [P, NT, N])
        region = sb("region", [P, 8192])
        xres = sb("xres", [P, NT, D])
        xagg = sb("xagg", [P, NT, D])
        xmoe = sb("xmoe", [P, NT, ROW])
        wide = sb("wide", [P, 2, GW])
        slot_in = sb("slot_in", [P, RING, ROW])
        slotT = sb("slotT", [P, 2, P])
        hbuf = sb("hbuf", [P, 4, F])
        slot_out = sb("slot_out", [P, RING, D])
        scratch = sb("scratch", [P, 464])
        ident = sb("ident", [P, P])
        before = sb("before", [P, P], bf16)
        ones = sb("ones", [P, P], bf16)
        segment = sb("segment", [P, E * C], bf16)
        fill_rows = sb("fill_rows", [P, ROW])
        iota_e = sb("iota_e", [P, E])
        iota_s = sb("iota_s", [P, SLOTS])
        base0 = sb("base0", [P, E])
        gnn_w = sb("gnn_w", [P, D])
        proj_w = sb("proj_w", [P, D])
        gcn_w = sb("gcn_w", [P, D])
        proj_b = sb("proj_b", [P, 1])
        gcn_b = sb("gcn_b", [P, 1])
        gate_w = [sb(f"gate_w{n}", [P, E]) for n in range(2)]
        gate_b = [sb(f"gate_b{n}", [P, E]) for n in range(2)]
        gamma = sb("gamma", [P, D])
        beta = sb("beta", [P, D])
        b2 = sb("b2", [E, D])
        b1T = sb("b1T", [P, FH, E])
        deg = sb("deg", [P, NT])
        dis = sb("dis", [P, NT])
        nnz = sb("nnz", [P, NT])
        over = sb("over", [P, NT])
        over_any = sb("over_any", [P, 1], bf16)
        flag = sb("flag", [1, 1], i32)
        neg_half = sb("neg_half", [P, GT])
        stats = sb("stats", [P, GT, 6])
        mv = sb("mv", [P, NT, 2])
        rstd = sb("rstd", [P, NT])
        shift = sb("shift", [P, NT])
        root_v = sb("root_v", [P, GT])
        root_t = sb("root_t", [P, GT])
        chosen = sb("chosen", [P, K, NT])
        gap = sb("gap", [P, NT])
        wsum = sb("wsum", [P, NT])
        wk = sb("wk", [P, K, NT])
        swap = sb("swap", [P, 2, NT])
        wrow = sb("wrow", [P, K, NT])
        base = sb("base", [P, E])
        pos = sb("pos", [P, K, NT], i32)
        count_i = sb("count_i", [P, E], i32)
        slots_f = sb("slots_f", [P, E])
        slots_end = sb("slots_end", [P, E])
        se_f = sb("se_f", [P, SLOTS])
        early = sb("early", [P, RING], i32)
        dest = sb("dest", [P, RING], i32)

        nat = region[:, 0:RING * N].rearrange("p (r n) -> p r n", r=RING)
        w1_0 = region[:, 0:E * F].rearrange("p (e f) -> p e f", e=E)
        w2_0 = region[:, E * F:2 * E * F].rearrange("p (e h d) -> p e h d", e=E, h=FH)
        w12_1 = region[:, 0:2 * E * F].rearrange("p (e w f) -> p e w f", e=E, w=2)
        w3_1 = adjT[:, 0:2, :].rearrange("p a n -> p (a n)").rearrange("p (e h d) -> p e h d", e=E, h=FH)
        silu = adjT[:, 2, 0:2 * F].rearrange("p (b f) -> p b f", b=2)
        tok = [region[:, 0:2 * N].rearrange("p (t k d) -> p t k d", t=NT, k=K),
               adjT[:, 4:6, :].rearrange("p a n -> p (a n)").rearrange("p (t k d) -> p t k d", t=NT, k=K)]
        exact = region[:, 0:N]
        remain = region[:, N:2 * N + 8]
        top8 = region[:, 2 * N + 8:2 * N + 16]

        tmpA = hbuf[:, 0:2, :].rearrange("p a f -> p (a f)")
        tmpB = hbuf[:, 2:4, :].rearrange("p a f -> p (a f)")
        slot_flat = slot_in[:, :, :].rearrange("p a f -> p (a f)")
        xnT = [slot_flat[:, 0:GW], slot_out[:, :, :].rearrange("p a f -> p (a f)")]
        b1_rows = slot_flat[0:E, 0:F]
        iota_i = slot_flat[:, F:F + 2 * E + SLOTS + NT].bitcast(i32)
        hmid = hbuf[:, 0:2, :]
        hidT = hbuf[:, 2:4, :]
        junkA = wide[:, :, :].rearrange("p a n -> p (a n)").bitcast(bf16)
        junkV = hbuf[:, :, :].rearrange("p a n -> p (a n)").bitcast(bf16)
        EC = E * C
        logits = scratch[:, 0:GT * E].rearrange("p (t e) -> p t e", t=GT)
        top = scratch[:, 64:96].rearrange("p (t n) -> p t n", t=GT)
        topi = scratch[:, 96:128].bitcast(u32).rearrange("p (t n) -> p t n", t=GT)
        onehot = scratch[:, 128:192].bitcast(bf16).rearrange("p (e k t) -> p e k t", e=E, k=K)
        tile_count = scratch[:, 192:192 + EC]
        running = scratch[:, 320:320 + EC]
        pos_f = scratch[:, 448:448 + C]
        ends = [tmpA[:, 0:SLOTS * E // 2].rearrange("p (s e) -> p s e", s=SLOTS),
                tmpB[:, 0:SLOTS * E // 2].rearrange("p (s e) -> p s e", s=SLOTS)]
        se_half = [tmpA[:, 384:384 + SLOTS], tmpB[:, 384:384 + SLOTS]]
        start_f = [scratch[:, 192:192 + SLOTS], scratch[:, 320:320 + SLOTS]]
        row_f = scratch[:, 256:256 + SLOTS]
        gates = tmpA[:, 0:NT * E].rearrange("p (t e) -> p t e", t=NT)
        gates_k = tmpB[:, 0:NT * E].rearrange("p (t e) -> p t e", t=NT)

        bank = [ctx.enter_context(nc.psum_tensor(f"bank{n}", [P, 512], f32)) for n in range(8)]

        dispatched = nc.dram_tensor("dispatched", (E * RUN, ROW), f32, kind="Internal").ap()
        expert_out = nc.dram_tensor("expert_out", (K * N, D), f32, kind="Internal").ap()

        def pair(name):
            return [sem(f"{name}{l}") for l in range(2)]

        x_in = sem("x_in")
        small_in = sem("small_in")
        nat_in = [sem(f"nat_in{n}") for n in range(RING)]
        weights_in = pair("weights_in")
        w3_in = sem("w3_in")
        pool_step = sem("pool_step")
        consts = sem("consts")
        dve_step = sem("dve_step")
        b1_turned = sem("b1_turned")
        b1_ready = sem("b1_ready")
        adj_turned = sem("adj_turned")
        adjT_dve = sem("adjT_dve")
        adjT_act = sem("adjT_act")
        deg_ready = sem("deg_ready")
        nnz_ready = sem("nnz_ready")
        xs_ready = sem("xs_ready")
        agg_done = pair("agg_done")
        agg_out = pair("agg_out")
        z_done = pair("z_done")
        z_used = pair("z_used")
        elu_min = sem("elu_min")
        elu_exp = sem("elu_exp")
        xn_ready = pair("xn_ready")
        xn_turned = pair("xn_turned")
        xnT_ready = pair("xnT_ready")
        logits_done = pair("logits_done")
        gap_ready = pair("gap_ready")
        gap_exp = pair("gap_exp")
        onehot_ready = pair("onehot_ready")
        ranks_done = pair("ranks_done")
        routed = pair("routed")
        runs_known = pair("runs_known")
        slots_known = pair("slots_known")
        scattered = pair("scattered")
        filled = pair("filled")
        gates_ready = sem("gates_ready")
        gates_turned = sem("gates_turned")
        gatesT_ready = sem("gatesT_ready")
        bias_done = sem("bias_done")
        bias_used = sem("bias_used")
        squared = sem("squared")
        filtered = sem("filtered")
        row_in = [[sem(f"row_in{l}_{n}") for n in range(RING)] for l in range(2)]
        row_turned = pair("row_turned")
        rowT_ready = pair("rowT_ready")
        early_ready = pair("early_ready")
        dest_ready = pair("dest_ready")
        up_done = pair("up_done")
        silu_ready = sem("silu_ready")
        hid_ready = pair("hid_ready")
        hid_turned = pair("hid_turned")
        hidT_ready = pair("hidT_ready")
        down_done = pair("down_done")
        out_ready = pair("out_ready")
        row_out = [[sem(f"row_out{l}_{n}") for n in range(RING)] for l in range(2)]
        tok_in = [[sem(f"tok_in{l}_{g}") for g in range(NG)] for l in range(2)]
        combined = pair("combined")
        mix_stats = sem("mix_stats")
        mix_scale = sem("mix_scale")
        mix_norm = sem("mix_norm")
        mixed = sem("mixed")
        xn1_stats = sem("xn1_stats")
        xn1_scale = sem("xn1_scale")
        xn1_ready = sem("xn1_ready")
        xn1_turned = sem("xn1_turned")
        xn1T_ready = sem("xn1T_ready")
        proj_done = sem("proj_done")
        h2_ready = sem("h2_ready")
        feat_done = sem("feat_done")
        feat_ready = sem("feat_ready")
        exact_in = sem("exact_in")
        exact_sq = sem("exact_sq")
        exact_tanh = sem("exact_tanh")
        exact_step = sem("exact_step")
        exact_kept = sem("exact_kept")
        exact_turned = sem("exact_turned")
        exact_used = sem("exact_used")
        stored = sem("stored")

        SMALL_LOADS = 13
        block = ctx.enter_context(nc.Block())

        def window(table, kind, s, lo, hi, largest):
            _, values = nc.values_load_multi_w_load_instructions(
                table[0:1, bass.ds(s + (LEAD + lo), hi - lo)], engines=[kind], min_val=0, max_val=largest,
                skip_runtime_bounds_check_because="the vector engine clamps the tables' entries")
            return values

        def run_slots(engine, step, depth, fetch=None):
            first = RING * (1 - (-depth // RING))
            last = RING * (SLOTS // RING)
            held = [None]

            def peeled(s):
                if fetch is not None and s % RING == 0:
                    held[0] = fetch(s)
                step(s, s, s, s // RING, s % RING, held[0])

            for s in range(first):
                peeled(s)
            with engine.Fori(first // RING, last // RING) as i:
                if fetch is not None:
                    held[0] = fetch(i * RING)
                for h in range(RING):
                    step(i * RING + h, first + h, last - RING + h, i, h, held[0])
            for s in range(last, SLOTS + depth):
                peeled(s)

        def live(lo, hi, back):
            return lo - back >= 0 and hi - back < SLOTS

        def rounds(i, h, back):
            return i + (h - back) // RING, (h - back) % RING

        @block.sync
        def _(sp):
            sp.dma_start(xres[:], x.rearrange("(t p) d -> p t d", p=P)).then_inc(x_in, 16)
            for r in range(RING):
                sp.dma_start(nat[:, r, :], adj[r * P:(r + 1) * P, :]).then_inc(nat_in[r], 16)
            with sp.Fori(1, NT // RING) as i:
                for r in range(RING):
                    sp.wait_ge(adj_turned, (i * RING + r - RING + 1) * GT)
                    sp.wait_ge(deg_ready, i * RING + r - RING + 1)
                    sp.wait_ge(nnz_ready, i * RING + r - RING + 1)
                    sp.dma_start(nat[:, r, :], adj[bass.ds((i * RING + r) * P, P), :]).then_inc(nat_in[r], 16)
            sp.wait_ge(adj_turned, NT * GT)
            sp.wait_ge(deg_ready, NT)
            sp.wait_ge(nnz_ready, NT)
            sp.dma_start(w1_0, L0_ffn_w1.rearrange("e d f -> d e f")).then_inc(weights_in[0], 16)
            sp.dma_start(w2_0, L0_ffn_w2.rearrange("e (h p) d -> p e h d", p=P)).then_inc(weights_in[0], 16)

            def slots(l):
                sp.wait_ge(consts, 1)
                sp.wait_ge(runs_known[l], 1)
                _, run_ends = nc.values_load_multi_w_load_instructions(
                    run_end[0:1, :], engines=[ENG.SP], min_val=0, max_val=E * RUN - P,
                    skip_runtime_bounds_check_because="an expert has at most N tokens of its run's N + P rows")
                for e in range(E):
                    sp.dma_start(dispatched[bass.ds(run_ends[e], P), :], fill_rows[:]).then_inc(filled[l], 16)

                def step(s, lo, hi, i, h, rows):
                    if live(lo, hi, 0):
                        if lo >= RING:
                            sp.wait_ge(row_turned[l], s - RING + 1)
                            sp.wait_ge(early_ready[l], s - RING + 1)
                        sp.dma_start(slot_in[:, h, :],
                                     dispatched[bass.ds(rows[h], P), :]).then_inc(row_in[l][h], 16)

                sp.wait_ge(slots_known[l], 1)
                sp.wait_ge(filled[l], 16 * E)
                sp.wait_ge(scattered[l], 16 * K * NT)
                run_slots(sp, step, 0, lambda s: window(slot_row, ENG.SP, s, 0, RING, E * RUN - P))
                for h in range(RING):
                    sp.wait_ge(row_out[l][h], 16 * len(range(h, SLOTS, RING)))
                for g in range(NG):
                    sp.dma_start(tok[l][:, g * GT:(g + 1) * GT, :, :].rearrange("p t k d -> p t (k d)"),
                                 expert_out[g * K * GW:(g + 1) * K * GW, :].rearrange(
                                     "(t p k) d -> p t (k d)", p=P, k=K)).then_inc(tok_in[l][g], 16)

            slots(0)
            sp.wait_ge(combined[0], NG)
            fl = sp.value_load(flag[0:1, 0:1], min_val=0, max_val=N)
            with sp.If(fl > 0):
                with sp.Fori(0, NT) as r:
                    sp.wait_ge(exact_used, r + 1)
                    sp.dma_start(exact, adj[bass.ds(r * P, P), :]).then_inc(exact_in, 16)
                sp.wait_ge(exact_used, NT + 1)
            sp.dma_start(w12_1[:, :, 0, :], L1_ffn_w1.rearrange("e d f -> d e f")).then_inc(weights_in[1], 16)
            sp.dma_start(w12_1[:, :, 1, :], L1_ffn_w2.rearrange("e d f -> d e f")).then_inc(weights_in[1], 16)
            sp.wait_ge(agg_done[1], NG)
            sp.dma_start(w3_1, L1_ffn_w3.rearrange("e (h p) d -> p e h d", p=P)).then_inc(w3_in, 16)
            slots(1)
            for g in range(NG):
                sp.wait_ge(combined[1], g + 1)
                sp.dma_start(out[g * GW:(g + 1) * GW, :].rearrange("(t p) d -> p t d", p=P),
                             xres[:, g * GT:(g + 1) * GT, :]).then_inc(stored, 16)
            sp.wait_ge(stored, 16 * NG)

        @block.gpsimd
        def _(pool):
            G = nc.gpsimd
            steps = Count(pool, pool_step)
            for ins in [
                G.memset(ident[:], 1.0), G.memset(ones[:], 1.0), G.memset(segment[:], 1.0),
                G.memset(fill_rows[:], 0.0), G.memset(neg_half[:], -0.5),
                G.memset(slot_expert[:], 0), G.memset(slot_row[:], 0),
                G.iota(iota_i[:, 0:E], pattern=[[1, E]], base=0, channel_multiplier=0),
                G.iota(iota_i[:, E:2 * E], pattern=[[RUN, E]], base=0, channel_multiplier=0),
                G.iota(iota_i[:, 2 * E:2 * E + SLOTS], pattern=[[1, SLOTS]], base=0, channel_multiplier=0),
                G.iota(iota_i[:, 2 * E + SLOTS:2 * E + SLOTS + NT], pattern=[[2 * P, NT]], base=0,
                       channel_multiplier=2),
            ]:
                steps.inc(ins)
            steps.wait()
            for ins in [
                G.affine_select(out=ident[:], in_=ident[:], compare_op=ALU.is_equal, fill=0.0,
                                base=0, pattern=[[-1, P]], channel_multiplier=1),
                G.affine_select(out=before[:], in_=ones[:], compare_op=ALU.is_gt, fill=0.0,
                                base=0, pattern=[[1, P]], channel_multiplier=-1),
                G.memset(segment[:, :].rearrange("p (e c) -> p e c", c=C)[:, :, 0:1], 0.0),
                G.memset(fill_rows[:, D:D + 1], NOBODY),
                G.tensor_copy(iota_e[:], iota_i[:, 0:E]),
                G.tensor_copy(base0[:], iota_i[:, E:2 * E]),
                G.tensor_copy(iota_s[:], iota_i[:, 2 * E:2 * E + SLOTS]),
                G.tensor_copy(xmoe[:, :, D], iota_i[:, 2 * E + SLOTS:2 * E + SLOTS + NT]),
            ]:
                steps.inc(ins)
            steps.wait()
            G.memset(flag[:], 0).then_inc(consts, 1)

            def send_tokens(l):
                for g in range(NG):
                    pool.wait_ge(routed[l], g + 1)
                    for t in range(g * GT, (g + 1) * GT):
                        for k in range(K):
                            G.indirect_dma_start(
                                out=dispatched, out_offset=bass.IndirectOffsetOnAxis(ap=pos[:, k, t:t + 1], axis=0),
                                in_=xmoe[:, t, :], in_offset=None).then_inc(scattered[l], 16)

            last_row = pool.to_reg(K * N - 1)

            def return_rows(l):
                def settle(s, lo, i, h):
                    pool.wait_ge(early_ready[l], s + 1)
                    if lo >= RING:
                        pool.wait_ge(row_out[l][h], 16 * i)
                    G.tensor_tensor(dest[:, h:h + 1], early[:, h:h + 1], fill_rows[:, 0:1].bitcast(i32),
                                    ALU.add).then_inc(dest_ready[l], 1)

                def step(s, lo, hi, i, h, _):
                    if live(lo, hi, 0):
                        pool.wait_ge(dest_ready[l], s + 1)
                        pool.wait_ge(out_ready[l], s + 1)
                    if live(lo, hi, -1):
                        settle(s + 1, lo + 1, *rounds(i, h, -1))
                    if live(lo, hi, 0):
                        G.indirect_dma_start(
                            out=expert_out, out_offset=bass.IndirectOffsetOnAxis(ap=dest[:, h:h + 1], axis=0),
                            in_=slot_out[:, h, :], in_offset=None, bounds_check=last_row,
                            oob_is_err=False).then_inc(row_out[l][h], 16)

                settle(0, 0, 0, 0)
                run_slots(pool, step, 0)

            def scale_and_shift(t0, signal):
                r, v = rstd[:, t0:t0 + GT], shift[:, t0:t0 + GT]
                steps.inc(G.tensor_scalar(v, mv[:, t0:t0 + GT, 1], EPS, None, ALU.add))
                steps.wait()
                steps.inc(G.tensor_tensor(r, v, neg_half[:], ALU.pow))
                steps.wait()
                steps.inc(G.tensor_tensor(v, mv[:, t0:t0 + GT, 0], r, ALU.mult))
                steps.wait()
                G.tensor_scalar(v, v, -1.0, None, ALU.mult).then_inc(signal, 1)

            send_tokens(0)
            return_rows(0)
            for s in range(NG + 1):
                if s < NG:
                    pool.wait_ge(mix_stats, s + 1)
                    scale_and_shift(s * GT, mix_scale)
                    pool.wait_ge(mix_norm, s + 1)
                    xg, yg = xres[:, s * GT:(s + 1) * GT, :], xagg[:, s * GT:(s + 1) * GT, :]
                    steps.inc(G.tensor_tensor(yg, yg, gamma[:, :].unsqueeze(1).to_broadcast([P, GT, D]), ALU.mult))
                    steps.wait()
                    steps.inc(G.tensor_tensor(yg, yg, beta[:, :].unsqueeze(1).to_broadcast([P, GT, D]), ALU.add))
                    steps.wait()
                    G.tensor_tensor(xg, yg, xg, ALU.add).then_inc(mixed, 1)
                if s >= 1:
                    pool.wait_ge(xn1_stats, s)
                    scale_and_shift((s - 1) * GT, xn1_scale)
            send_tokens(1)
            return_rows(1)

        @block.scalar
        def _(act):
            for dst, src in [
                (b1_rows, L0_ffn_b1),
                (gnn_w[:], L0_gnn_w), (proj_w[:], L1_gnn_W_proj), (gcn_w[:], L1_gnn_W_gcn),
                (proj_b[:], L1_gnn_b_proj.unsqueeze(1)), (gcn_b[:], L1_gnn_b_gcn.unsqueeze(1)),
                (gate_w[0][:], L0_ffn_gate_w), (gate_w[1][:], L1_ffn_gate_w),
                (gate_b[0][:], L0_ffn_gate_b.partition_broadcast(P)),
                (gate_b[1][:], L1_ffn_gate_b.partition_broadcast(P)),
                (gamma[:], L0_ffn_gamma.partition_broadcast(P)), (beta[:], L0_ffn_beta.partition_broadcast(P)),
                (b2[:], L0_ffn_b2),
            ]:
                act.dma_start(dst, src).then_inc(small_in, 16)

            with act.Fori(0, NT // RING) as i:
                for r in range(RING):
                    act.wait_ge(nat_in[r], (i + 1) * 16)
                    nc.scalar.activation(junkA, nat[:, r, :], ACT.Copy,
                                         accum_out=deg[:, bass.ds(i * RING + r, 1)]).then_inc(deg_ready, 1)
                    for q in (2, 3):
                        act.wait_ge(adj_turned, (i * RING + r) * GT + q + 1)
                        nc.scalar.copy(adjT[:, q * GT:(q + 1) * GT, bass.ds((i * RING + r) * P, P)],
                                       bank[4 + q][:, :].rearrange("p (a b) -> p a b", a=GT)).then_inc(adjT_act, 1)
                    act.wait_ge(deg_ready, i * RING + r + 1)

            def after_aggregation(l):
                for s in range(NG + 2):
                    if s < NG:
                        act.wait_ge(agg_done[l], s + 1)
                        if s >= 2:
                            act.wait_ge(z_done[l], s - 1)
                        if l == 0:
                            nc.scalar.copy(wide[:, s % 2, :], bank[s][:]).then_inc(agg_out[l], 1)
                        else:
                            nc.scalar.activation(wide[:, s % 2, :], bank[s][:], ACT.Relu,
                                                 bias=gcn_b[:, 0:1]).then_inc(agg_out[l], 1)
                    if 1 <= s <= NG and l == 0:
                        act.wait_ge(elu_min, s)
                        nc.scalar.activation(tmpB, tmpB, ACT.Exp).then_inc(elu_exp, 1)
                    if s >= 2:
                        xnT_out(l, s - 2)
                act.wait_ge(gap_ready[l], NG)
                nc.scalar.activation(gap[:], gap[:], ACT.Exp).then_inc(gap_exp[l], 1)

            def xnT_out(l, g):
                act.wait_ge(xn_turned[l], g + 1)
                if g >= 2:
                    act.wait_ge(logits_done[l], g - 1)
                nc.scalar.copy(xnT[g % 2], bank[6 + g % 2][:]).then_inc(xnT_ready[l], 1)

            def filter_group(g):
                for j in range(0, NT, GT):
                    a = adjT[:, j:j + GT, g * GW:(g + 1) * GW]
                    act.wait_ge(squared, g * NG + j // GT + 1)
                    nc.scalar.activation(a, a, ACT.Tanh).then_inc(filtered, 1)

            after_aggregation(0)
            for g in range(NG):
                act.wait_ge(gates_turned, g + 1)
                if g >= 2:
                    act.wait_ge(bias_done, g - 1)
                nc.scalar.copy(wide[0:E, g % 2, :], bank[4 + g % 2][0:E, :]).then_inc(gatesT_ready, 1)

            def row_to_send(l, s, lo, i, h):
                ri, rh = rounds(i, h, 3)
                act.wait_ge(down_done[l], s - 3 + 1)
                if lo - 3 >= RING:
                    act.wait_ge(row_out[l][rh], 16 * ri)
                nc.scalar.copy(slot_out[:, rh, :], bank[6 + (h - 3) % 2][:, 0:D]).then_inc(out_ready[l], 1)

            def step0(s, lo, hi, i, h, experts):
                if live(lo, hi, 3):
                    row_to_send(0, s, lo, i, h)
                if live(lo, hi, 2):
                    act.wait_ge(hid_turned[0], s - 2 + 1)
                    pt = bank[4 + (h - 2) % 2]
                    for f in range(FH):
                        last = nc.scalar.activation(hidT[:, (h - 2) % 2, f * P:(f + 1) * P], pt[:, f * P:(f + 1) * P],
                                                    ACT.Relu, bias=b1T[:, f, bass.ds(experts[RING + h - 2], 1)])
                    last.then_inc(hidT_ready[0], 1)

            act.wait_ge(slots_known[0], 1)
            act.wait_ge(b1_ready, 1)
            run_slots(act, step0, 3, lambda s: window(slot_expert, ENG.Activation, s, -RING, RING, E - 1))

            filter_group(0)

            def normalize(g, scale, signal):
                act.wait_ge(scale, g + 1)
                for t in range(g * GT, (g + 1) * GT):
                    last = nc.scalar.activation(xagg[:, t, :], (xagg if signal is mix_norm else xres)[:, t, :],
                                                ACT.Identity, bias=shift[:, t:t + 1], scale=rstd[:, t:t + 1])
                last.then_inc(signal, 1)

            for s in range(NG + 1):
                if s < NG:
                    normalize(s, mix_scale, mix_norm)
                if s >= 1:
                    g = s - 1
                    normalize(g, xn1_scale, xn1_ready)
                    act.wait_ge(xn1_turned, g + 1)
                    nc.scalar.copy(wide[:, 0, :], bank[4][:]).then_inc(xn1T_ready, 1)
                    act.wait_ge(proj_done, g + 1)
                    nc.scalar.activation(wide[:, 1, :], bank[5][:], ACT.Tanh, bias=proj_b[:, 0:1]).then_inc(h2_ready, 1)
                    act.wait_ge(feat_done, g + 1)
                    nc.scalar.copy(xagg[:, g * GT:(g + 1) * GT, :],
                                   bank[6][:, :].rearrange("p (a b) -> p a b", a=GT)).then_inc(feat_ready, 1)

            for g in range(1, NG):
                filter_group(g)
            fl = act.value_load(flag[0:1, 0:1], min_val=0, max_val=N)
            with act.If(fl > 0):
                with act.Fori(0, NT) as r:
                    act.wait_ge(exact_sq, r + 1)
                    nc.scalar.activation(exact, exact, ACT.Tanh).then_inc(exact_tanh, 1)

            after_aggregation(1)

            def step1(s, lo, hi, i, h, _):
                if live(lo, hi, 3):
                    row_to_send(1, s, lo, i, h)
                if live(lo, hi, 1):
                    b = (h - 1) % 2
                    act.wait_ge(up_done[1], s - 1 + 1)
                    if lo - 1 >= 2:
                        act.wait_ge(hid_ready[1], s - 1 - 1)
                    nc.scalar.activation(silu[:, b, :], bank[2 + b][:, 0:F], ACT.Silu).then_inc(silu_ready, 1)

            run_slots(act, step1, 3)

        @block.vector
        def _(dve):
            V = nc.vector
            steps = Count(dve, dve_step)

            def run(ins):
                steps.inc(ins)
                steps.wait()

            def rsqrt(y, v, add):
                run(V.tensor_scalar(root_v[:], v, add, None, ALU.add))
                run(V.tensor_scalar(y.bitcast(i32), root_v[:, :].bitcast(i32), -0.5, float(0x5F3759DF),
                                    ALU.mult, ALU.add))
                for _ in range(3):
                    run(V.tensor_tensor(root_t[:], y, y, ALU.mult))
                    run(V.scalar_tensor_tensor(out=root_t[:], in0=root_t[:], scalar=-0.5, in1=root_v[:],
                                               op0=ALU.mult, op1=ALU.mult))
                    run(V.scalar_tensor_tensor(out=y, in0=root_t[:], scalar=1.5, in1=y,
                                               op0=ALU.add, op1=ALU.mult))

            def layer_stats(src, t0, signal=None):
                for t in range(GT):
                    steps.inc(V.bn_stats(stats[:, t, :], src[:, t0 + t, :]))
                steps.wait()
                for t in range(GT):
                    last = V.bn_aggr(mv[:, t0 + t, :], stats[:, t, :])
                    if signal is None or t < GT - 1:
                        steps.inc(last)
                    else:
                        last.then_inc(signal, 1)
                steps.wait()
                if signal is not None:
                    dve.wait_ge(signal, t0 // GT + 1)

            def layer_shift(t0):
                run(V.scalar_tensor_tensor(out=shift[:, t0:t0 + GT], in0=mv[:, t0:t0 + GT, 0], scalar=-1.0,
                                           in1=rstd[:, t0:t0 + GT], op0=ALU.mult, op1=ALU.mult))

            def apply(dst, src, t0, signal):
                for t in range(t0, t0 + GT):
                    last = V.tensor_scalar(dst[:, t, 0:D], src[:, t, :], rstd[:, t:t + 1], shift[:, t:t + 1],
                                           ALU.mult, ALU.add)
                last.then_inc(signal, 1)

            def input_stats(g):
                layer_stats(xres, g * GT)
                rsqrt(rstd[:, g * GT:(g + 1) * GT], mv[:, g * GT:(g + 1) * GT, 1], EPS)

            dve.wait_ge(x_in, 16)
            input_stats(0)

            for g in range(NG):
                for r in range(RING):
                    t = g * RING + r
                    dve.wait_ge(nat_in[r], (g + 1) * 16)
                    V.tensor_scalar(junkV, nat[:, r, :], 0.0, 0.0, ALU.is_gt, ALU.add,
                                    accum_out=nnz[:, t:t + 1]).then_inc(nnz_ready, 1)
                    for q in (0, 1):
                        dve.wait_ge(adj_turned, t * GT + q + 1)
                        V.tensor_copy(adjT[:, q * GT:(q + 1) * GT, t * P:(t + 1) * P],
                                      bank[4 + q][:, :].rearrange("p (a b) -> p a b", a=GT)).then_inc(adjT_dve, 1)
                    dve.wait_ge(nnz_ready, t + 1)
                t0 = g * GT
                dve.wait_ge(deg_ready, t0 + GT)
                rsqrt(dis[:, t0:t0 + GT], deg[:, t0:t0 + GT], 1.0)
                run(V.tensor_tensor(rstd[:, t0:t0 + GT], rstd[:, t0:t0 + GT], dis[:, t0:t0 + GT], ALU.mult))
                layer_shift(t0)
                apply(xagg, xres, t0, xs_ready)
                if g < NG - 1:
                    input_stats(g + 1)

            run(V.tensor_scalar(over[:], nnz[:], float(TOP), None, ALU.is_gt))
            steps.inc(V.tensor_reduce(over_any[:], over[:], AX, ALU.max))
            dve.wait_ge(b1_turned, 1)
            V.tensor_copy(b1T[:, :, :], bank[4][:, 0:FH * E].rearrange("p (f e) -> p f e", f=FH)).then_inc(b1_ready, 1)

            def graph_to_residual(l, g):
                t0 = g * GT
                xg = xres[:, t0:t0 + GT, :]
                z = bank[4 + g % 2][:, :].rearrange("p (t d) -> p t d", t=GT)
                A3 = tmpA.rearrange("p (t d) -> p t d", t=GT)
                dve.wait_ge(z_done[l], g + 1)
                if l == 1:
                    V.tensor_tensor(xg, z, xg, ALU.add).then_inc(z_used[l], 1)
                    dve.wait_ge(z_used[l], g + 1)
                    return
                V.tensor_tensor(A3, z, dis[:, t0:t0 + GT].unsqueeze(2).to_broadcast([P, GT, D]),
                                ALU.mult).then_inc(z_used[l], 1)
                dve.wait_ge(z_used[l], g + 1)
                V.tensor_scalar(tmpB, tmpA, 0.0, None, ALU.min).then_inc(elu_min, 1)
                dve.wait_ge(elu_exp, g + 1)
                run(V.scalar_tensor_tensor(out=tmpA, in0=tmpA, scalar=0.0, in1=tmpB, op0=ALU.max, op1=ALU.add))
                run(V.scalar_tensor_tensor(out=xg, in0=A3, scalar=-1.0, in1=xg, op0=ALU.add, op1=ALU.add))

            def gate_group(l, g):
                t0 = g * GT
                dve.wait_ge(logits_done[l], g + 1)
                run(V.tensor_tensor(logits, bank[g][:, 0:GT * E].rearrange("p (t e) -> p t e", t=GT),
                                    gate_b[l][:, :].unsqueeze(1).to_broadcast([P, GT, E]), ALU.add))
                for t in range(GT):
                    steps.inc(V.max(out=top[:, t, :], in_=logits[:, t, :]))
                steps.wait()
                for t in range(GT):
                    steps.inc(V.max_index(out=topi[:, t, :], in_max=top[:, t, :], in_values=logits[:, t, :]))
                steps.wait()
                steps.inc(V.tensor_copy(chosen[:, :, t0:t0 + GT], topi[:, :, 0:K].rearrange("p t k -> p k t")))
                steps.wait()
                for k in range(K):
                    V.tensor_tensor(onehot[:, :, k, :], iota_e[:, :].unsqueeze(2).to_broadcast([P, E, GT]),
                                    chosen[:, k, t0:t0 + GT].unsqueeze(1).to_broadcast([P, E, GT]),
                                    ALU.is_equal).then_inc(onehot_ready[l], 1)
                V.tensor_tensor(gap[:, t0:t0 + GT], top[:, :, 1], top[:, :, 0], ALU.subtract).then_inc(gap_ready[l], 1)
                steps.inc(V.tensor_tensor(xmoe[:, t0:t0 + GT, D + 1], chosen[:, 0, t0:t0 + GT],
                                          chosen[:, 1, t0:t0 + GT], ALU.max))

            def rank_group(l, g):
                t0 = g * GT
                earlier, counts = bank[g][:, 128:128 + EC], bank[g][:, 256:256 + EC]
                dve.wait_ge(ranks_done[l], g + 1)
                dve.wait_ge(onehot_ready[l], K * (g + 1))
                run(V.tensor_copy(tile_count, counts))
                by_expert = tile_count.rearrange("p (e c) -> p e c", c=C)
                run(V.tensor_tensor(by_expert[:, :, 0], by_expert[:, :, 0], base[:], ALU.add))
                run(V.tensor_tensor_scan(running, segment[:], tile_count, 0.0, ALU.mult, ALU.add))
                steps.inc(V.tensor_copy(base[:], running.rearrange("p (e c) -> p e c", c=C)[:, :, C - 1]))
                run(V.tensor_tensor(tile_count, running, counts, ALU.subtract))
                run(V.tensor_tensor(running, tile_count, earlier, ALU.add))
                run(V.tensor_tensor(tile_count, running, onehot.rearrange("p e k t -> p (e k t)"), ALU.mult))
                run(V.tensor_reduce(pos_f, tile_count.rearrange("p (e c) -> p c e", c=C), AX, ALU.add))
                V.tensor_copy(pos[:, :, t0:t0 + GT], pos_f.rearrange("p (k t) -> p k t", k=K)).then_inc(routed[l], 1)

            def after_aggregation(l):
                run(V.tensor_copy(base[:], base0[:]))
                for s in range(NG + 2):
                    if s < NG:
                        graph_to_residual(l, s)
                        layer_stats(xres, s * GT)
                        rsqrt(rstd[:, s * GT:(s + 1) * GT], mv[:, s * GT:(s + 1) * GT, 1], EPS)
                        layer_shift(s * GT)
                        apply(xmoe, xres, s * GT, xn_ready[l])
                    if s >= 2:
                        rank_group(l, s - 2)
                    if 1 <= s <= NG:
                        gate_group(l, s - 1)

            def plan_slots(l):
                V.tensor_copy(run_end[0:1, :], base[0:1, :]).then_inc(runs_known[l], 1)
                run(V.tensor_tensor(slots_f[:], base[:], base0[:], ALU.subtract))
                run(V.tensor_copy(count_i[:], slots_f[:]))
                run(V.tensor_scalar(count_i[:], count_i[:], P - 1, None, ALU.add))
                run(V.tensor_scalar(count_i[:], count_i[:], P.bit_length() - 1, None, ALU.arith_shift_right))
                run(V.tensor_copy(slots_f[:], count_i[:]))
                run(V.tensor_tensor_scan(slots_end[:], ones[:, 0:E], slots_f[:], 0.0, ALU.mult, ALU.add))
                for half in range(2):
                    part = slice(half * E // 2, (half + 1) * E // 2)
                    steps.inc(V.tensor_tensor(ends[half], slots_end[:, part].unsqueeze(1).to_broadcast([P, SLOTS, E // 2]),
                                              iota_s[:, :].unsqueeze(2).to_broadcast([P, SLOTS, E // 2]), ALU.is_le))
                steps.wait()
                for half in range(2):
                    steps.inc(V.tensor_reduce(se_half[half], ends[half], AX, ALU.add))
                steps.wait()
                for half in range(2):
                    part = slice(half * E // 2, (half + 1) * E // 2)
                    steps.inc(V.tensor_tensor(ends[half], ends[half],
                                              slots_f[:, part].unsqueeze(1).to_broadcast([P, SLOTS, E // 2]), ALU.mult))
                steps.wait()
                for half in range(2):
                    steps.inc(V.tensor_reduce(start_f[half], ends[half], AX, ALU.add))
                run(V.tensor_tensor(se_f[:], se_half[0], se_half[1], ALU.add))
                run(V.tensor_tensor(start_f[0], start_f[0], start_f[1], ALU.add))
                run(V.tensor_tensor(start_f[0], iota_s[:], start_f[0], ALU.subtract))
                steps.inc(V.tensor_scalar(row_f, se_f[:], float(RUN), None, ALU.mult))
                steps.wait()
                run(V.scalar_tensor_tensor(out=row_f, in0=start_f[0], scalar=float(P), in1=row_f,
                                           op0=ALU.mult, op1=ALU.add))
                run(V.tensor_scalar(row_f, row_f, base[:, E - 1:E], None, ALU.min))
                run(V.tensor_scalar(se_f[:], se_f[:], float(E - 1), None, ALU.min))
                run(V.tensor_copy(slot_row[0:1, LEAD:LEAD + SLOTS], row_f[0:1, :]))
                V.tensor_copy(slot_expert[0:1, LEAD:LEAD + SLOTS], se_f[0:1, :]).then_inc(slots_known[l], 1)

            def token_weights(l):
                dve.wait_ge(gap_exp[l], 1)
                run(V.tensor_scalar(wsum[:], gap[:], 1.0, None, ALU.add))
                run(V.reciprocal(wk[:, 0, :], wsum[:]))
                run(V.tensor_tensor(wk[:, 1, :], wk[:, 0, :], gap[:], ALU.mult))
                steps.inc(V.tensor_tensor(swap[:, 0, :], chosen[:, 0, :], chosen[:, 1, :], ALU.is_gt))
                steps.inc(V.tensor_tensor(swap[:, 1, :], chosen[:, 0, :], chosen[:, 1, :], ALU.is_le))
                steps.wait()
                for k in range(K):
                    run(V.tensor_tensor(wsum[:], swap[:, 1 - k, :], wk[:, 0, :], ALU.mult))
                    run(V.tensor_tensor(wrow[:, k, :], swap[:, k, :], wk[:, 1, :], ALU.mult))
                    run(V.tensor_tensor(wrow[:, k, :], wrow[:, k, :], wsum[:], ALU.add))

            def square_group(g):
                for j in range(0, NT, GT):
                    a = adjT[:, j:j + GT, g * GW:(g + 1) * GW]
                    V.scalar_tensor_tensor(out=a, in0=a, scalar=0.0, in1=a, op0=ALU.max,
                                           op1=ALU.mult).then_inc(squared, 1)

            def combine(l, g, acc):
                dve.wait_ge(tok_in[l][g], 16)
                for k in range(K):
                    for t in range(g * GT, (g + 1) * GT):
                        last = V.scalar_tensor_tensor(out=acc[:, t, :], in0=tok[l][:, t, k, :],
                                                      scalar=wrow[:, k, t:t + 1], in1=acc[:, t, :],
                                                      op0=ALU.mult, op1=ALU.add)
                        if k == K - 1 and t == (g + 1) * GT - 1:
                            last.then_inc(combined[l], 1)
                        else:
                            steps.inc(last)
                    if k == 0:
                        steps.wait()
                steps.wait()
                dve.wait_ge(combined[l], g + 1)

            after_aggregation(0)
            dve.wait_ge(ranks_done[0], NG)
            steps.inc(V.tensor_copy(flag[0:1, 0:1], bank[3][0:1, 400:401]))
            plan_slots(0)
            token_weights(0)
            for k in range(K):
                run(V.tensor_tensor(gates_k, iota_e[:, :].unsqueeze(1).to_broadcast([P, NT, E]),
                                    chosen[:, k, :].unsqueeze(2).to_broadcast([P, NT, E]), ALU.is_equal))
                if k == 0:
                    run(V.tensor_tensor(gates, gates_k, wk[:, k, :].unsqueeze(2).to_broadcast([P, NT, E]), ALU.mult))
                else:
                    run(V.tensor_tensor(gates_k, gates_k, wk[:, k, :].unsqueeze(2).to_broadcast([P, NT, E]), ALU.mult))
                    V.tensor_tensor(gates, gates, gates_k, ALU.add).then_inc(gates_ready, 1)
            for g in range(NG):
                dve.wait_ge(bias_done, g + 1)
                V.tensor_tensor(xagg[:, g * GT:(g + 1) * GT, :], bank[6 + g % 2][:, :].rearrange("p (t d) -> p t d", t=GT),
                                xmoe[:, g * GT:(g + 1) * GT, 0:D], ALU.add).then_inc(bias_used, 1)

            def row_arrived(l, s, lo, i, h):
                dve.wait_ge(row_turned[l], s + 1)
                V.tensor_copy(slotT[:, h % 2, :], bank[h % 2][:, 0:P]).then_inc(rowT_ready[l], 1)
                dve.wait_ge(row_in[l][h], 16 * (i + 1))
                if lo >= RING:
                    dve.wait_ge(dest_ready[l], s - RING + 1)
                V.scalar_tensor_tensor(out=early[:, h:h + 1], in0=slot_in[:, h, D + 1:D + 2],
                                       scalar=se_f[:, bass.ds(s, 1)], in1=slot_in[:, h, D:D + 1],
                                       op0=ALU.is_equal, op1=ALU.add).then_inc(early_ready[l], 1)

            def step0(s, lo, hi, i, h, _):
                if live(lo, hi, 1):
                    b = (h - 1) % 2
                    dve.wait_ge(up_done[0], s - 1 + 1)
                    V.tensor_copy(hmid[:, b, :], bank[2 + b][:, 0:F]).then_inc(hid_ready[0], 1)
                if live(lo, hi, 0):
                    row_arrived(0, s, lo, i, h)

            run_slots(dve, step0, 1)
            square_group(0)

            for s in range(NG + 1):
                if s < NG:
                    combine(0, s, xagg)
                    layer_stats(xagg, s * GT, mix_stats)
                if s >= 1:
                    dve.wait_ge(mixed, s)
                    layer_stats(xres, (s - 1) * GT, xn1_stats)
            for g in range(1, NG):
                square_group(g)

            fl = dve.value_load(flag[0:1, 0:1], min_val=0, max_val=N)
            with dve.If(fl > 0):
                dve.wait_ge(filtered, NG * NG)
                rounds_full, rest = TOP // 8, TOP % 8
                V.memset(over[:, 0:1], 0.0).then_inc(exact_used, 1)
                with dve.Fori(0, NT) as r:
                    per = 3 + 2 * rounds_full + 3
                    k = [0]

                    def chained(ins):
                        ins.then_inc(exact_step, 1)
                        k[0] += 1
                        dve.wait_ge(exact_step, r * per + k[0])
                        V.memset(over[:, 1:2], 0.0)

                    dve.wait_ge(exact_in, (r + 1) * 16)
                    V.scalar_tensor_tensor(out=exact, in0=exact, scalar=0.0, in1=exact, op0=ALU.max,
                                           op1=ALU.mult).then_inc(exact_sq, 1)
                    dve.wait_ge(exact_tanh, r + 1)
                    chained(V.tensor_copy(remain[:, 0:N], exact))
                    chained(V.memset(remain[:, N:N + 8], -1.0))
                    for _ in range(rounds_full):
                        chained(V.max(out=top8, in_=remain))
                        chained(V.match_replace(out=remain, in_to_replace=top8, in_values=remain, imm_value=0.0))
                    chained(V.max(out=top8, in_=remain))
                    chained(V.memset(top8[:, rest:8], -1.0))
                    chained(V.match_replace(out=remain, in_to_replace=top8, in_values=remain, imm_value=0.0))
                    chained(V.tensor_tensor(remain[:, 0:N], exact, remain[:, 0:N], ALU.subtract))
                    assert k[0] == per
                    for q in range(GT):
                        dve.wait_ge(exact_turned, r * GT + q + 1)
                        V.tensor_copy(adjT[:, q * GT:(q + 1) * GT, bass.ds(r * P, P)],
                                      bank[4 + q % 2][:, :].rearrange("p (a b) -> p a b", a=GT)).then_inc(exact_kept, 1)
                    dve.wait_ge(exact_kept, (r + 1) * GT)
                    V.memset(over[:, 0:1], 0.0).then_inc(exact_used, 1)

            after_aggregation(1)
            plan_slots(1)
            token_weights(1)

            def step1(s, lo, hi, i, h, _):
                if live(lo, hi, 2):
                    b = (h - 2) % 2
                    dve.wait_ge(hid_turned[1], s - 2 + 1)
                    V.tensor_copy(hidT[:, b, :], bank[4 + b][:, 0:F]).then_inc(hidT_ready[1], 1)
                if live(lo, hi, 1):
                    b = (h - 1) % 2
                    dve.wait_ge(silu_ready, s - 1 + 1)
                    V.tensor_tensor(hmid[:, b, :], silu[:, b, :], bank[2 + b][:, F:2 * F],
                                    ALU.mult).then_inc(hid_ready[1], 1)
                if live(lo, hi, 0):
                    row_arrived(1, s, lo, i, h)

            run_slots(dve, step1, 2)
            for g in range(NG):
                combine(1, g, xres)

        @block.tensor
        def _(pe):
            T = nc.tensor
            pe.wait_ge(consts, 1)

            def products(g, tiles, first, last):
                return [lambda j=j: T.matmul(bank[g][:], xagg[:, j, :], adjT[:, j, g * GW:(g + 1) * GW],
                                             start=(j == first), stop=(j == last)) for j in tiles]

            def adj_rows(g, beside):
                for r in range(RING):
                    t = g * RING + r
                    pe.wait_ge(nat_in[r], (g + 1) * 16)
                    for q in range(GT):
                        if t >= 1:
                            pe.wait_ge(adjT_dve if q < 2 else adjT_act, 2 * (t - 1) + q % 2 + 1)
                        for b in range(GT):
                            last = T.transpose(bank[4 + q][:, b * P:(b + 1) * P],
                                               nat[:, r, (q * GT + b) * P:(q * GT + b + 1) * P], ident[:])
                        last.then_inc(adj_turned, 1)
                        at = r * GT + q
                        if at == 0 and beside:
                            all_in(g - 1)
                        for go in beside[at * len(beside) // 16:(at + 1) * len(beside) // 16]:
                            go()

            def all_in(g):
                pe.wait_ge(adjT_dve, 2 * (g + 1) * RING)
                pe.wait_ge(adjT_act, 2 * (g + 1) * RING)
                pe.wait_ge(xs_ready, g + 1)

            beside = []
            for g in range(NG):
                adj_rows(g, beside)
                beside = [go for i in range(g + 1)
                          for go in products(i, range(0 if i == g else g * GT, (g + 1) * GT), 0, NT)]
            all_in(NG - 1)

            def finish_aggregation(l, g):
                if l == 1:
                    pe.wait_ge(filtered, NG * (g + 1))
                if l == 1 or g == NG - 1:
                    todo = products(g, range(NT), 0, NT - 1)
                else:
                    todo = products(g, range(NT - GT, NT), 0, NT - 1)
                for go in todo[:-1]:
                    go()
                if l == 0:
                    for b in range(GT):
                        T.matmul(bank[g][:, b * P:(b + 1) * P], xagg[:, g * GT + b, :], ident[:], start=False, stop=False)
                todo[-1]().then_inc(agg_done[l], 1)

            def to_token_major(l, g):
                pe.wait_ge(agg_out[l], g + 1)
                if g >= 2:
                    pe.wait_ge(z_used[l], g - 1)
                for b in range(GT):
                    o, a = bank[4 + g % 2][:, b * P:(b + 1) * P], wide[:, g % 2, b * P:(b + 1) * P]
                    last = T.matmul(o, a, gnn_w[:], start=True, stop=True) if l == 0 else T.transpose(o, a, ident[:])
                last.then_inc(z_done[l], 1)

            def gate_logits(l, g):
                pe.wait_ge(xn_ready[l], g + 1)
                if g >= 2:
                    pe.wait_ge(xnT_ready[l], g - 1)
                for b in range(GT):
                    last = T.transpose(bank[6 + g % 2][:, b * P:(b + 1) * P], xmoe[:, g * GT + b, 0:D], ident[:])
                last.then_inc(xn_turned[l], 1)
                pe.wait_ge(xnT_ready[l], g + 1)
                for b in range(GT):
                    last = T.matmul(bank[g][:, b * E:(b + 1) * E], xnT[g % 2][:, b * P:(b + 1) * P], gate_w[l][:],
                                    start=True, stop=True)
                last.then_inc(logits_done[l], 1)

            def count_ranks(l, g):
                m = onehot.rearrange("p e k t -> p (e k t)")
                pe.wait_ge(onehot_ready[l], K * (g + 1))
                T.matmul(bank[g][:, 128:128 + EC], before[:], m, start=True, stop=True)
                if l == 0 and g == NG - 1:
                    T.matmul(bank[g][:, 400:401], ones[:], over_any[:], start=True, stop=True)
                T.matmul(bank[g][:, 256:256 + EC], ones[:], m, start=True, stop=True).then_inc(ranks_done[l], 1)

            def graph_layer_end(l):
                for s in range(NG + 3):
                    if s < NG:
                        finish_aggregation(l, s)
                    if s == 0 and l == 0:
                        pe.wait_ge(small_in, 16 * SMALL_LOADS)
                        for f in range(FH):
                            last = T.transpose(bank[4][:, f * E:(f + 1) * E], b1_rows[:, f * P:(f + 1) * P],
                                               ident[0:E, 0:E])
                        last.then_inc(b1_turned, 1)
                        pe.wait_ge(b1_ready, 1)
                    if 1 <= s <= NG:
                        to_token_major(l, s - 1)
                    if 2 <= s <= NG + 1:
                        gate_logits(l, s - 2)
                    if s >= 3:
                        count_ranks(l, s - 3)

            def slots(l):
                w_up = w1_0 if l == 0 else w12_1.rearrange("p e w f -> p e (w f)")
                w_down = w2_0 if l == 0 else w3_1
                up = F if l == 0 else 2 * F

                def step(s, lo, hi, i, h, experts):
                    if live(lo, hi, 3):
                        b = (h - 3) % 2
                        pe.wait_ge(hidT_ready[l], s - 3 + 1)
                        if lo - 3 >= 2:
                            pe.wait_ge(out_ready[l], s - 3 - 1)
                        for f in range(FH):
                            last = T.matmul(bank[6 + b][:, 0:D], hidT[:, b, f * P:(f + 1) * P],
                                            w_down[:, bass.ds(experts[RING + h - 3], 1), f, :],
                                            start=(f == 0), stop=(f == FH - 1))
                        last.then_inc(down_done[l], 1)
                    if live(lo, hi, 2):
                        b = (h - 2) % 2
                        pe.wait_ge(hid_ready[l], s - 2 + 1)
                        if lo - 2 >= 2:
                            pe.wait_ge(hidT_ready[l], s - 2 - 1)
                        for f in range(FH):
                            last = T.transpose(bank[4 + b][:, f * P:(f + 1) * P], hmid[:, b, f * P:(f + 1) * P], ident[:])
                        last.then_inc(hid_turned[l], 1)
                    if live(lo, hi, 1):
                        b = (h - 1) % 2
                        pe.wait_ge(rowT_ready[l], s - 1 + 1)
                        if lo - 1 >= 2:
                            pe.wait_ge(hid_ready[l], s - 1 - 1)
                        T.matmul(bank[2 + b][:, 0:up], slotT[:, b, :], w_up[:, bass.ds(experts[RING + h - 1], 1), :],
                                 start=True, stop=True).then_inc(up_done[l], 1)
                    if live(lo, hi, 0):
                        pe.wait_ge(row_in[l][h], 16 * (i + 1))
                        if lo >= 2:
                            pe.wait_ge(rowT_ready[l], s - 1)
                        T.transpose(bank[h % 2][:, 0:P], slot_in[:, h, 0:D], ident[:]).then_inc(row_turned[l], 1)

                pe.wait_ge(slots_known[l], 1)
                if l == 0:
                    pe.wait_ge(weights_in[0], 16 * 2)
                else:
                    pe.wait_ge(weights_in[1], 16 * 2)
                    pe.wait_ge(w3_in, 16)
                run_slots(pe, step, 3, lambda s: window(slot_expert, ENG.PE, s, -RING, RING, E - 1))

            graph_layer_end(0)
            for g in range(NG + 1):
                if g < NG:
                    pe.wait_ge(gates_ready, 1)
                    if g >= 2:
                        pe.wait_ge(gatesT_ready, g - 1)
                    for b in range(GT):
                        last = T.matmul(bank[4 + g % 2][0:E, b * P:(b + 1) * P], gates[:, g * GT + b, :], ident[:],
                                        start=True, stop=True)
                    last.then_inc(gates_turned, 1)
                if g >= 1:
                    pe.wait_ge(gatesT_ready, g)
                    if g >= 3:
                        pe.wait_ge(bias_used, g - 2)
                    for b in range(GT):
                        last = T.matmul(bank[6 + (g - 1) % 2][:, b * P:(b + 1) * P],
                                        wide[0:E, (g - 1) % 2, b * P:(b + 1) * P], b2[:], start=True, stop=True)
                    last.then_inc(bias_done, 1)
            slots(0)

            for g in range(NG):
                pe.wait_ge(xn1_ready, g + 1)
                for b in range(GT):
                    last = T.transpose(bank[4][:, b * P:(b + 1) * P], xagg[:, g * GT + b, :], ident[:])
                last.then_inc(xn1_turned, 1)
                pe.wait_ge(xn1T_ready, g + 1)
                T.matmul(bank[5][:], proj_w[:], wide[:, 0, :], start=True, stop=True).then_inc(proj_done, 1)
                pe.wait_ge(h2_ready, g + 1)
                if g >= 1:
                    pe.wait_ge(feat_ready, g)
                for b in range(GT):
                    last = T.matmul(bank[6][:, b * P:(b + 1) * P], wide[:, 1, b * P:(b + 1) * P], gcn_w[:],
                                    start=True, stop=True)
                last.then_inc(feat_done, 1)
            pe.wait_ge(feat_ready, NG)
            fl = pe.value_load(flag[0:1, 0:1], min_val=0, max_val=N)
            with pe.If(fl > 0):
                with pe.Fori(0, NT) as r:
                    pe.wait_ge(exact_step, (r + 1) * (3 + 2 * (TOP // 8) + 3))
                    for q in range(GT):
                        if q >= 2:
                            pe.wait_ge(exact_kept, r * GT + q - 1)
                        for b in range(GT):
                            last = T.transpose(bank[4 + q % 2][:, b * P:(b + 1) * P],
                                               remain[:, (q * GT + b) * P:(q * GT + b + 1) * P], ident[:])
                        last.then_inc(exact_turned, 1)
                    pe.wait_ge(exact_kept, (r + 1) * GT)

            graph_layer_end(1)
            slots(1)


_INS = ['x', 'adj', 'L0_gnn_w', 'L0_ffn_gate_w', 'L0_ffn_gate_b', 'L0_ffn_w1', 'L0_ffn_b1', 'L0_ffn_w2', 'L0_ffn_b2',
        'L0_ffn_gamma', 'L0_ffn_beta', 'L1_gnn_W_proj', 'L1_gnn_b_proj', 'L1_gnn_W_gcn', 'L1_gnn_b_gcn',
        'L1_ffn_gate_w', 'L1_ffn_gate_b', 'L1_ffn_w1', 'L1_ffn_w2', 'L1_ffn_w3']
_OUTS = [((2048, 128), 'float32')]


def kernel(**inputs):
    import numpy as _np
    import concourse.bacc as _bacc
    from concourse import mybir as _mybir
    from concourse.bass_utils import run_bass_kernel_spmd as _run

    nc = _bacc.Bacc("TRN2", target_bir_lowering=False, num_devices=1)
    arrays, args = {}, []
    for name in _INS:
        a = _np.ascontiguousarray(inputs[name])
        arrays[f"in_{name}_dram"] = a
        args.append(nc.dram_tensor(f"in_{name}_dram", a.shape, _mybir.dt.from_np(a.dtype), kind="ExternalInput").ap())
    for i, (shape, dtype) in enumerate(_OUTS):
        dt = _mybir.dt.from_np(_np.dtype(dtype))
        args.append(nc.dram_tensor(f"out_{i}_dram", shape, dt, kind="ExternalOutput").ap())
    gnn_moe_gnn_moe_kernel(nc, *args)
    r = _run(nc, [arrays], core_ids=[0])
    return r.results[0]["out_0_dram"]
```

```python
import concourse.bass as bass
from concourse import mybir
from contextlib import ExitStack


class Count:

    def __init__(self, engine, sem):
        self.engine, self.sem, self.n = engine, sem, 0

    def inc(self, instruction):
        instruction.then_inc(self.sem, 1)
        self.n += 1

    def wait(self):
        self.engine.wait_ge(self.sem, self.n)


def gnn_moe_gnn_moe_kernel(
    nc: bass.Bass,
    x: bass.AP,
    adj: bass.AP,
    L0_gnn_w: bass.AP,
    L0_ffn_gate_w: bass.AP,
    L0_ffn_gate_b: bass.AP,
    L0_ffn_w1: bass.AP,
    L0_ffn_b1: bass.AP,
    L0_ffn_w2: bass.AP,
    L0_ffn_b2: bass.AP,
    L0_ffn_gamma: bass.AP,
    L0_ffn_beta: bass.AP,
    L1_gnn_W_proj: bass.AP,
    L1_gnn_b_proj: bass.AP,
    L1_gnn_W_gcn: bass.AP,
    L1_gnn_b_gcn: bass.AP,
    L1_ffn_gate_w: bass.AP,
    L1_ffn_gate_b: bass.AP,
    L1_ffn_w1: bass.AP,
    L1_ffn_w2: bass.AP,
    L1_ffn_w3: bass.AP,
    out: bass.AP,
):
    f32, bf16 = mybir.dt.float32, mybir.dt.bfloat16
    i32, u32 = mybir.dt.int32, mybir.dt.uint32
    ALU = mybir.AluOpType
    ACT = mybir.ActivationFunctionType
    ENG = mybir.EngineType
    AX = mybir.AxisListType.X

    P = 128
    N, D = x.shape
    E, _, F = L0_ffn_w1.shape
    NT = N // P
    GT = 4
    NG = NT // GT
    GW = GT * P
    K = 2
    TOP = 350
    EPS = 1e-5
    C = K * GT
    RUN = N + P
    SLOTS = (K * N + E * (P - 1)) // P
    MAIN = K * N // P + E // 2 + 2
    RING = 4
    FH = F // P
    ROW = D + 2
    NOBODY = float(2 ** 20)
    LEAD = 8
    UP, DOWN = 2, 4
    UNROLL = 2 * RING
    LOOP_FROM = -(-(DOWN + RING) // UNROLL) * UNROLL
    LOOP_TO = MAIN // UNROLL * UNROLL
    FILTER_FROM, FILTER_TO = DOWN, MAIN - 1
    PIECES = FILTER_TO - FILTER_FROM
    PIECE = 3 * NT * N // (4 * PIECES) // 32 * 32
    LATE_PIECES = 8
    LATE_PIECE = (NT * N - PIECES * PIECE) // LATE_PIECES
    assert PIECES * PIECE + LATE_PIECES * LATE_PIECE == NT * N

    ctx = ExitStack()
    with ctx:
        def sb(name, shape, dt=f32):
            return ctx.enter_context(nc.sbuf_tensor(name, shape, dt))

        def sem(name):
            return ctx.enter_context(nc.semaphore(name))

        slot_expert = sb("slot_expert", [1, 80], i32)
        slot_row = sb("slot_row", [1, 80], i32)
        run_end = sb("run_end", [1, E], i32)
        adjT = sb("adjT", [P, NT, N])
        region = sb("region", [P, 8192])
        xres = sb("xres", [P, NT, D])
        xagg = sb("xagg", [P, NT, D])
        xmoe = sb("xmoe", [P, NT, ROW])
        wide = sb("wide", [P, 2, GW])
        slot_in = sb("slot_in", [P, RING, ROW])
        slotT = sb("slotT", [P, 2, P])
        hbuf = sb("hbuf", [P, 4, F])
        slot_out = sb("slot_out", [P, RING, D])
        scratch = sb("scratch", [P, 464])
        ident = sb("ident", [P, P])
        not_before = sb("not_before", [P, P], bf16)
        ones = sb("ones", [P, P], bf16)
        segment = sb("segment", [P, E * C], bf16)
        fill_rows = sb("fill_rows", [P, ROW])
        iota_e = sb("iota_e", [P, E])
        iota_s = sb("iota_s", [P, SLOTS])
        base0 = sb("base0", [P, E])
        gnn_w = sb("gnn_w", [P, D])
        proj_w = sb("proj_w", [P, D])
        gcn_w = sb("gcn_w", [P, D])
        proj_b = sb("proj_b", [P, 1])
        gcn_b = sb("gcn_b", [P, 1])
        gate_w = [sb(f"gate_w{n}", [P, E]) for n in range(2)]
        gate_b = [sb(f"gate_b{n}", [P, E]) for n in range(2)]
        gamma = sb("gamma", [P, D])
        beta = sb("beta", [P, D])
        b2 = sb("b2", [E, D])
        b1T = sb("b1T", [P, FH, E])
        deg = sb("deg", [P, NT])
        dis = sb("dis", [P, NT])
        nnz = sb("nnz", [P, NT])
        over = sb("over", [P, NT])
        over_any = sb("over_any", [P, 1], bf16)
        flag = sb("flag", [1, 1], i32)
        beyond = sb("beyond", [1, 1], i32)
        neg_half = sb("neg_half", [P, GT])
        carrier = sb("carrier", [P, 2])
        stats = sb("stats", [P, GT, 6])
        mv = sb("mv", [P, NT, 2])
        rstd = sb("rstd", [P, NT])
        shift = sb("shift", [P, NT])
        root_v = sb("root_v", [P, GT])
        root_t = sb("root_t", [P, GT])
        chosen = sb("chosen", [P, K, NT])
        gap = sb("gap", [P, NT])
        wsum = sb("wsum", [P, NT])
        wk = sb("wk", [P, K, NT])
        swap = sb("swap", [P, 2, NT])
        wrow = sb("wrow", [P, K, NT])
        base = sb("base", [P, E])
        pos = sb("pos", [P, K, NT], i32)
        count_i = sb("count_i", [P, E], i32)
        slots_f = sb("slots_f", [P, E])
        slots_end = sb("slots_end", [P, E])
        se_f = sb("se_f", [P, SLOTS])
        early = sb("early", [P, SLOTS], i32)
        dest = sb("dest", [P, RING], i32)

        nat = region[:, 0:RING * N].rearrange("p (r n) -> p r n", r=RING)
        up_w = [region[:, 0:RING * F].rearrange("p (r f) -> p r f", r=RING),
                adjT[:, 8, :].rearrange("p (r f) -> p r f", r=RING)]
        w12_1 = region[:, 0:2 * E * F].rearrange("p (e w f) -> p e w f", e=E, w=2)
        w2_0 = region[:, E * F:2 * E * F].rearrange("p (e h d) -> p e h d", e=E, h=FH)
        w3_1 = adjT[:, 0:2, :].rearrange("p a n -> p (a n)").rearrange("p (e h d) -> p e h d", e=E, h=FH)
        silu = adjT[:, 2, 0:2 * F].rearrange("p (b f) -> p b f", b=2)
        tok = [region[:, 0:2 * N].rearrange("p (t k d) -> p t k d", t=NT, k=K),
               adjT[:, 4:6, :].rearrange("p a n -> p (a n)").rearrange("p (t k d) -> p t k d", t=NT, k=K)]
        exact = region[:, 0:N]
        remain = region[:, N:2 * N + 8]
        top8 = region[:, 2 * N + 8:2 * N + 16]

        adj_flat = adjT[:, :, :].rearrange("p t n -> p (t n)")
        tmpA = hbuf[:, 0:2, :].rearrange("p a f -> p (a f)")
        tmpB = hbuf[:, 2:4, :].rearrange("p a f -> p (a f)")
        slot_flat = slot_in[:, :, :].rearrange("p a f -> p (a f)")
        xnT = [slot_flat[:, 0:GW], slot_out[:, :, :].rearrange("p a f -> p (a f)")]
        b1_rows = slot_flat[0:E, 0:F]
        iota_i = slot_flat[:, F:F + 2 * E + SLOTS + NT].bitcast(i32)
        hidT = hbuf[:, 2:4, :]
        junkA = wide[:, :, :].rearrange("p a n -> p (a n)").bitcast(bf16)
        junkV = hbuf[:, :, :].rearrange("p a n -> p (a n)").bitcast(bf16)
        EC = E * C
        logits = scratch[:, 0:GT * E].rearrange("p (t e) -> p t e", t=GT)
        top = scratch[:, 64:96].rearrange("p (t n) -> p t n", t=GT)
        topi = scratch[:, 96:128].bitcast(u32).rearrange("p (t n) -> p t n", t=GT)
        onehot = scratch[:, 128:192].bitcast(bf16).rearrange("p (e k t) -> p e k t", e=E, k=K)
        tile_rank = scratch[:, 192:192 + EC]
        by_expert = tile_rank.rearrange("p (e c) -> p e c", c=C)
        running = scratch[:, 320:320 + EC]
        pos_f = scratch[:, 448:448 + C]
        ends = [tmpA[:, 0:SLOTS * E // 2].rearrange("p (s e) -> p s e", s=SLOTS),
                tmpB[:, 0:SLOTS * E // 2].rearrange("p (s e) -> p s e", s=SLOTS)]
        se_half = [tmpA[:, 384:384 + SLOTS], tmpB[:, 384:384 + SLOTS]]
        start_f = [scratch[:, 192:192 + SLOTS], scratch[:, 320:320 + SLOTS]]
        row_f = scratch[:, 256:256 + SLOTS]
        gates = xnT[1][:, 0:NT * E].rearrange("p (t e) -> p t e", t=NT)
        gates_k = tmpB[:, 0:NT * E].rearrange("p (t e) -> p t e", t=NT)

        bank = [ctx.enter_context(nc.psum_tensor(f"bank{n}", [P, 512], f32)) for n in range(8)]

        dispatched = nc.dram_tensor("dispatched", (E * RUN, ROW), f32, kind="Internal").ap()
        expert_out = nc.dram_tensor("expert_out", (K * N, D), f32, kind="Internal").ap()

        def pair(name):
            return [sem(f"{name}{l}") for l in range(2)]

        x_in = sem("x_in")
        small_in = sem("small_in")
        nat_in = [sem(f"nat_in{n}") for n in range(RING)]
        up_w_in = [[sem(f"up_w_in{l}_{n}") for n in range(RING)] for l in range(2)]
        all_up_w_in = sem("all_up_w_in")
        down_w_in = pair("down_w_in")
        pool_step = sem("pool_step")
        consts = sem("consts")
        dve_step = sem("dve_step")
        b1_turned = sem("b1_turned")
        b1_ready = sem("b1_ready")
        adj_turned = sem("adj_turned")
        adjT_dve = sem("adjT_dve")
        adjT_act = sem("adjT_act")
        deg_ready = sem("deg_ready")
        nnz_ready = sem("nnz_ready")
        xs_ready = sem("xs_ready")
        input_stats_ready = sem("input_stats_ready")
        agg_done = pair("agg_done")
        agg_out = pair("agg_out")
        z_done = pair("z_done")
        z_used = sem("z_used")
        elu_parts = sem("elu_parts")
        elu_used = sem("elu_used")
        stats_ready = pair("stats_ready")
        xs_scale = sem("xs_scale")
        xn_ready = pair("xn_ready")
        xn_turned = pair("xn_turned")
        xnT_ready = pair("xnT_ready")
        logits_done = pair("logits_done")
        gap_ready = pair("gap_ready")
        gap_exp = pair("gap_exp")
        onehot_ready = pair("onehot_ready")
        ranks_done = pair("ranks_done")
        routed = pair("routed")
        runs_known = pair("runs_known")
        slots_known = pair("slots_known")
        scattered = pair("scattered")
        filled = pair("filled")
        gates_ready = sem("gates_ready")
        gates_turned = sem("gates_turned")
        gatesT_ready = sem("gatesT_ready")
        bias_done = sem("bias_done")
        bias_used = sem("bias_used")
        squared = sem("squared")
        filtered = sem("filtered")
        row_in = [[sem(f"row_in{l}_{n}") for n in range(RING)] for l in range(2)]
        row_turned = pair("row_turned")
        rowT_ready = pair("rowT_ready")
        early_ready = pair("early_ready")
        dest_ready = pair("dest_ready")
        up_done = pair("up_done")
        silu_ready = sem("silu_ready")
        hidT_ready = pair("hidT_ready")
        down_done = pair("down_done")
        out_ready = pair("out_ready")
        row_out = [[sem(f"row_out{l}_{n}") for n in range(RING)] for l in range(2)]
        tok_in = [[sem(f"tok_in{l}_{g}") for g in range(NG)] for l in range(2)]
        combined = pair("combined")
        mix_stats = sem("mix_stats")
        mix_scale = sem("mix_scale")
        xn1_stats = sem("xn1_stats")
        xn1_scale = sem("xn1_scale")
        xn1_ready = sem("xn1_ready")
        xn1_turned = sem("xn1_turned")
        xn1T_ready = sem("xn1T_ready")
        proj_done = sem("proj_done")
        h2_ready = sem("h2_ready")
        feat_done = sem("feat_done")
        feat_ready = sem("feat_ready")
        exact_in = sem("exact_in")
        exact_sq = sem("exact_sq")
        exact_tanh = sem("exact_tanh")
        exact_step = sem("exact_step")
        exact_kept = sem("exact_kept")
        exact_turned = sem("exact_turned")
        exact_used = sem("exact_used")
        stored = sem("stored")
        x_finished = pair("x_finished")
        x_free, x_row_in, x_up_w_in, x_row_turned, x_rowT_ready, x_early, x_up_done, x_silu, x_hidT_ready, \
            x_down_done, x_out_ready, x_dest, x_may_send, x_row_out = [sem(f"x_{n}") for n in (
                "free", "row_in", "up_w_in", "row_turned", "rowT_ready", "early", "up_done", "silu", "hidT_ready",
                "down_done", "out_ready", "dest", "may_send", "row_out")]

        SMALL_LOADS = 13
        block = ctx.enter_context(nc.Block())

        def piece(k):
            return adj_flat[:, bass.ds(k * PIECE, PIECE)]

        def late_piece(k):
            first = PIECES * PIECE + k * LATE_PIECE
            return adj_flat[:, first:first + LATE_PIECE]

        def window(table, kind, s, lo, hi, largest):
            _, values = nc.values_load_multi_w_load_instructions(
                table[0:1, bass.ds(s + (LEAD + lo), hi - lo)], engines=[kind], min_val=0, max_val=largest,
                skip_runtime_bounds_check_because="the vector engine clamps the tables' entries")
            return values

        def run_slots(engine, step, depth, fetch=None):
            held = [None]

            def one(s, lo, hi, i, h):
                step(s, lo, hi, i, h % RING, held[0] and held[0][h % UNROLL:])

            def peeled(s):
                if fetch is not None and s % UNROLL == 0:
                    held[0] = fetch(s)
                one(s, s, s, s // RING, s % UNROLL)

            for s in range(LOOP_FROM):
                peeled(s)
            with engine.Fori(LOOP_FROM // UNROLL, LOOP_TO // UNROLL) as i:
                if fetch is not None:
                    held[0] = fetch(i * UNROLL)
                for h in range(UNROLL):
                    one(i * UNROLL + h, LOOP_FROM + h, LOOP_TO - UNROLL + h, i * (UNROLL // RING) + h // RING, h)
            for s in range(LOOP_TO, MAIN + depth):
                peeled(s)

        def live(lo, hi, back):
            return lo - back >= 0 and hi - back < MAIN

        def rounds(i, h, back):
            return i + (h - back) // RING, (h - back) % RING

        def is_beyond(engine):
            return engine.value_load(beyond[0:1, 0:1], min_val=0, max_val=1)

        def free_count(k, more):
            return k + 1 if len(more) == 1 else k + 1 + more[0]

        def beyond_main(engine, more, step):
            with engine.If(more[-1] > 0):
                with engine.Fori(MAIN, SLOTS) as s:
                    step(s, s - MAIN if len(more) == 1 else s - MAIN + more[0] * (SLOTS - MAIN))

        @block.sync
        def _(sp):
            more = []
            for r in range(RING):
                sp.dma_start(nat[:, r, :], adj[r * P:(r + 1) * P, :]).then_inc(nat_in[r], 16)
                if r == 0:
                    sp.dma_start(xres[:], x.rearrange("(t p) d -> p t d", p=P)).then_inc(x_in, 16)
            for dst, src in [
                (b1_rows, L0_ffn_b1),
                (gnn_w[:], L0_gnn_w), (proj_w[:], L1_gnn_W_proj), (gcn_w[:], L1_gnn_W_gcn),
                (proj_b[:], L1_gnn_b_proj.unsqueeze(1)), (gcn_b[:], L1_gnn_b_gcn.unsqueeze(1)),
                (gate_w[0][:], L0_ffn_gate_w), (gate_w[1][:], L1_ffn_gate_w),
                (gate_b[0][:], L0_ffn_gate_b.partition_broadcast(P)),
                (gate_b[1][:], L1_ffn_gate_b.partition_broadcast(P)),
                (gamma[:], L0_ffn_gamma.partition_broadcast(P)), (beta[:], L0_ffn_beta.partition_broadcast(P)),
                (b2[:], L0_ffn_b2),
            ]:
                sp.dma_start(dst, src).then_inc(small_in, 16)
            with sp.Fori(1, NT // RING) as i:
                for r in range(RING):
                    sp.wait_ge(adj_turned, (i * RING + r - RING + 1) * GT)
                    sp.wait_ge(deg_ready, i * RING + r - RING + 1)
                    sp.wait_ge(nnz_ready, i * RING + r - RING + 1)
                    sp.dma_start(nat[:, r, :], adj[bass.ds((i * RING + r) * P, P), :]).then_inc(nat_in[r], 16)
            sp.wait_ge(adj_turned, NT * GT)
            sp.wait_ge(deg_ready, NT)
            sp.wait_ge(nnz_ready, NT)
            sp.dma_start(w2_0, L0_ffn_w2.rearrange("e (h p) d -> p e h d", p=P)).then_inc(down_w_in[0], 16)

            def slots(l):
                sp.wait_ge(consts, 1)
                sp.wait_ge(runs_known[l], 1)
                _, run_ends = nc.values_load_multi_w_load_instructions(
                    run_end[0:1, :], engines=[ENG.SP], min_val=0, max_val=E * RUN - P,
                    skip_runtime_bounds_check_because="an expert has at most N tokens of its run's N + P rows")
                for e in range(E):
                    sp.dma_start(dispatched[bass.ds(run_ends[e], P), :], fill_rows[:]).then_inc(filled[l], 16)

                def step(s, lo, hi, i, h, rows):
                    if hi == 0:
                        sp.wait_ge(filled[l], 16 * E)
                        sp.wait_ge(scattered[l], 16 * K * NT)
                    if live(lo, hi, 0):
                        if lo >= RING:
                            sp.wait_ge(row_turned[l], s - RING + 1)
                            sp.wait_ge(early_ready[l], s - RING + 1)
                        sp.dma_start(slot_in[:, h, :],
                                     dispatched[bass.ds(rows[0], P), :]).then_inc(row_in[l][h], 16)

                sp.wait_ge(slots_known[l], 1)
                fl = sp.value_load(flag[0:1, 0:1], min_val=0, max_val=N) if l == 0 else None
                more.append(is_beyond(sp))
                run_slots(sp, step, 0, lambda s: window(slot_row, ENG.SP, s, 0, UNROLL, E * RUN - P))
                for h in range(RING):
                    sp.wait_ge(row_out[l][h], 16 * len(range(h, MAIN, RING)))

                def one_more(s, k):
                    sp.wait_ge(x_free, free_count(k, more))
                    row, = window(slot_row, ENG.SP, s, 0, 1, E * RUN - P)
                    expert, = window(slot_expert, ENG.SP, s, 0, 1, E - 1)
                    sp.dma_start(slot_in[:, 0, :], dispatched[bass.ds(row, P), :]).then_inc(x_row_in, 16)
                    w = L0_ffn_w1.rearrange("e d f -> d e f") if l == 0 else w12_1.rearrange("p e w f -> p e (w f)")
                    sp.dma_start(up_w[l][:, 0:1, :], w[:, bass.ds(expert, 1), :]).then_inc(x_up_w_in, 16)

                beyond_main(sp, more, one_more)
                with sp.If(more[-1] > 0):
                    sp.wait_ge(x_finished[l], 1)
                if l == 0:
                    with sp.If(fl > 0):
                        with sp.Fori(0, NT) as r:
                            sp.wait_ge(exact_used, r + 1)
                            sp.dma_start(exact, adj[bass.ds(r * P, P), :]).then_inc(exact_in, 16)
                        sp.wait_ge(exact_used, NT + 1)
                for g in range(NG):
                    sp.dma_start(tok[l][:, g * GT:(g + 1) * GT, :, :].rearrange("p t k d -> p t (k d)"),
                                 expert_out[g * K * GW:(g + 1) * K * GW, :].rearrange(
                                     "(t p k) d -> p t (k d)", p=P, k=K)).then_inc(tok_in[l][g], 16)

            slots(0)
            sp.wait_ge(combined[0], NG)
            sp.dma_start(w12_1[:, :, 0, :], L1_ffn_w1.rearrange("e d f -> d e f")).then_inc(all_up_w_in, 16)
            sp.dma_start(w12_1[:, :, 1, :], L1_ffn_w2.rearrange("e d f -> d e f")).then_inc(all_up_w_in, 16)
            sp.wait_ge(agg_done[1], NG)
            sp.dma_start(w3_1, L1_ffn_w3.rearrange("e (h p) d -> p e h d", p=P)).then_inc(down_w_in[1], 16)
            slots(1)
            for g in range(NG):
                sp.wait_ge(combined[1], g + 1)
                sp.dma_start(out[g * GW:(g + 1) * GW, :].rearrange("(t p) d -> p t d", p=P),
                             xres[:, g * GT:(g + 1) * GT, :]).then_inc(stored, 16)
            sp.wait_ge(stored, 16 * NG)

        @block.gpsimd
        def _(pool):
            more = []
            G = nc.gpsimd
            steps = Count(pool, pool_step)
            for ins in [
                G.memset(ident[:], 1.0), G.memset(ones[:], 1.0), G.memset(segment[:], 1.0),
                G.memset(fill_rows[:], 0.0), G.memset(neg_half[:], -0.5), G.memset(not_before[:], -1.0),
                G.memset(slot_expert[:], 0), G.memset(slot_row[:], 0),
                G.iota(iota_i[:, 0:E], pattern=[[1, E]], base=0, channel_multiplier=0),
                G.iota(iota_i[:, E:2 * E], pattern=[[RUN, E]], base=0, channel_multiplier=0),
                G.iota(iota_i[:, 2 * E:2 * E + SLOTS], pattern=[[1, SLOTS]], base=0, channel_multiplier=0),
                G.iota(iota_i[:, 2 * E + SLOTS:2 * E + SLOTS + NT], pattern=[[2 * P, NT]], base=0,
                       channel_multiplier=2),
            ]:
                steps.inc(ins)
            steps.wait()
            for ins in [
                G.affine_select(out=ident[:], in_=ident[:], compare_op=ALU.is_equal, fill=0.0,
                                base=0, pattern=[[-1, P]], channel_multiplier=1),
                G.affine_select(out=not_before[:], in_=not_before[:], compare_op=ALU.is_ge, fill=0.0,
                                base=0, pattern=[[-1, P]], channel_multiplier=1),
                G.memset(segment[:, :].rearrange("p (e c) -> p e c", c=C)[:, :, 0:1], 0.0),
                G.memset(fill_rows[:, D:D + 1], NOBODY),
                G.tensor_copy(iota_e[:], iota_i[:, 0:E]),
                G.tensor_copy(base0[:], iota_i[:, E:2 * E]),
                G.tensor_copy(iota_s[:], iota_i[:, 2 * E:2 * E + SLOTS]),
                G.tensor_copy(xmoe[:, :, D], iota_i[:, 2 * E + SLOTS:2 * E + SLOTS + NT]),
            ]:
                steps.inc(ins)
            steps.wait()
            G.memset(flag[:], 0).then_inc(consts, 1)

            def send_tokens(l):
                for g in range(NG):
                    pool.wait_ge(routed[l], g + 1)
                    for t in range(g * GT, (g + 1) * GT):
                        for k in range(K):
                            G.indirect_dma_start(
                                out=dispatched, out_offset=bass.IndirectOffsetOnAxis(ap=pos[:, k, t:t + 1], axis=0),
                                in_=xmoe[:, t, :], in_offset=None).then_inc(scattered[l], 16)

            last_row = pool.to_reg(K * N - 1)

            def return_rows(l):
                pool.wait_ge(slots_known[l], 1)

                def settle(s, lo, i, h):
                    pool.wait_ge(early_ready[l], s + 1)
                    if lo >= RING:
                        pool.wait_ge(row_out[l][h], 16 * i)
                    G.tensor_tensor(dest[:, h:h + 1], early[:, bass.ds(s, 1)], fill_rows[:, 0:1].bitcast(i32),
                                    ALU.add).then_inc(dest_ready[l], 1)

                def step(s, lo, hi, i, h, _):
                    if live(lo, hi, 0):
                        pool.wait_ge(dest_ready[l], s + 1)
                        pool.wait_ge(out_ready[l], s + 1)
                    if live(lo, hi, -1):
                        settle(s + 1, lo + 1, *rounds(i, h, -1))
                    if live(lo, hi, 0):
                        G.indirect_dma_start(
                            out=expert_out, out_offset=bass.IndirectOffsetOnAxis(ap=dest[:, h:h + 1], axis=0),
                            in_=slot_out[:, h, :], in_offset=None, bounds_check=last_row,
                            oob_is_err=False).then_inc(row_out[l][h], 16)

                def carry(cell, signal):
                    G.tensor_tensor(carrier[:, cell:cell + 1], fill_rows[:, 0:1], fill_rows[:, 0:1],
                                    ALU.add).then_inc(signal, 1)

                def one_more(s, k):
                    pool.wait_ge(x_free, free_count(k, more))
                    pool.wait_ge(x_early, k + 1)
                    G.tensor_tensor(dest[:, 0:1], early[:, bass.ds(s, 1)], fill_rows[:, 0:1].bitcast(i32),
                                    ALU.add).then_inc(x_dest, 1)
                    pool.wait_ge(x_dest, k + 1)
                    pool.wait_ge(x_out_ready, k + 1)
                    carry(0, x_may_send)
                    G.indirect_dma_start(
                        out=expert_out, out_offset=bass.IndirectOffsetOnAxis(ap=dest[:, 0:1], axis=0),
                        in_=slot_out[:, 0, :], in_offset=None, bounds_check=last_row,
                        oob_is_err=False).then_inc(x_row_out, 16)
                    pool.wait_ge(x_may_send, k + 1)
                    pool.wait_ge(x_row_out, 16 * (k + 1))
                    carry(1, x_free)

                more.append(is_beyond(pool))
                settle(0, 0, 0, 0)
                run_slots(pool, step, 0)
                with pool.If(more[-1] > 0):
                    for h in range(RING):
                        pool.wait_ge(row_out[l][h], 16 * len(range(h, MAIN, RING)))
                    carry(1, x_free)
                beyond_main(pool, more, one_more)
                with pool.If(more[-1] > 0):
                    done = SLOTS - MAIN
                    pool.wait_ge(x_free, free_count(done if l == 0 else more[0] * done + done, more))
                    carry(0, x_finished[l])

            def scale_and_shift(t0, signal):
                r, v = rstd[:, t0:t0 + GT], shift[:, t0:t0 + GT]
                steps.inc(G.tensor_scalar(v, mv[:, t0:t0 + GT, 1], EPS, None, ALU.add))
                steps.wait()
                steps.inc(G.tensor_tensor(r, v, neg_half[:], ALU.pow))
                steps.wait()
                steps.inc(G.tensor_tensor(v, mv[:, t0:t0 + GT, 0], r, ALU.mult))
                steps.wait()
                G.tensor_scalar(v, v, -1.0, None, ALU.mult).then_inc(signal, 1)

            for g in range(NG):
                r, d, m = (a[:, g * GT:(g + 1) * GT] for a in (rstd, dis, shift))
                pool.wait_ge(input_stats_ready, g + 1)
                steps.inc(G.tensor_scalar(m, mv[:, g * GT:(g + 1) * GT, 1], EPS, None, ALU.add))
                steps.wait()
                steps.inc(G.tensor_tensor(r, m, neg_half[:], ALU.pow))
                pool.wait_ge(deg_ready, (g + 1) * GT)
                steps.inc(G.tensor_scalar(d, deg[:, g * GT:(g + 1) * GT], 1.0, None, ALU.add))
                steps.wait()
                steps.inc(G.tensor_tensor(d, d, neg_half[:], ALU.pow))
                steps.wait()
                steps.inc(G.tensor_tensor(r, r, d, ALU.mult))
                steps.wait()
                steps.inc(G.tensor_tensor(m, mv[:, g * GT:(g + 1) * GT, 0], r, ALU.mult))
                steps.wait()
                G.tensor_scalar(m, m, -1.0, None, ALU.mult).then_inc(xs_scale, 1)
            send_tokens(0)
            pool.wait_ge(xn_ready[0], NG)
            for g in range(NG):
                xg = xres[:, g * GT:(g + 1) * GT, :]
                steps.inc(G.tensor_tensor(xg, xg, beta[:, :].unsqueeze(1).to_broadcast([P, GT, D]), ALU.add))
            steps.wait()
            return_rows(0)
            for g in range(NG):
                pool.wait_ge(mix_stats, g + 1)
                r, v = rstd[:, g * GT:(g + 1) * GT], shift[:, g * GT:(g + 1) * GT]
                steps.inc(G.tensor_scalar(v, mv[:, g * GT:(g + 1) * GT, 1], EPS, None, ALU.add))
                steps.wait()
                G.tensor_tensor(r, v, neg_half[:], ALU.pow).then_inc(mix_scale, 1)
                pool.wait_ge(mix_scale, g + 1)
                pool.wait_ge(xn1_stats, g + 1)
                scale_and_shift(g * GT, xn1_scale)
            send_tokens(1)
            return_rows(1)

        @block.scalar
        def _(act):
            more = []
            with act.Fori(0, NT // RING) as i:
                for r in range(RING):
                    act.wait_ge(nat_in[r], (i + 1) * 16)
                    nc.scalar.activation(junkA, nat[:, r, :], ACT.Copy,
                                         accum_out=deg[:, bass.ds(i * RING + r, 1)]).then_inc(deg_ready, 1)
                    for q in (2, 3):
                        act.wait_ge(adj_turned, (i * RING + r) * GT + q + 1)
                        nc.scalar.copy(adjT[:, q * GT:(q + 1) * GT, bass.ds((i * RING + r) * P, P)],
                                       bank[4 + q][:, :].rearrange("p (a b) -> p a b", a=GT)).then_inc(adjT_act, 1)
                    act.wait_ge(deg_ready, i * RING + r + 1)

            def aggregated_out(l, g):
                act.wait_ge(agg_done[l], g + 1)
                if g >= 2:
                    act.wait_ge(z_done[l], g - 1)
                if l == 0:
                    nc.scalar.copy(wide[:, g % 2, :], bank[g][:]).then_inc(agg_out[l], 1)
                else:
                    nc.scalar.activation(wide[:, g % 2, :], bank[g][:], ACT.Relu,
                                         bias=gcn_b[:, 0:1]).then_inc(agg_out[l], 1)

            def elu_halves(l, g):
                if l == 1:
                    return
                act.wait_ge(z_done[l], g + 1)
                if g >= 1:
                    act.wait_ge(elu_used, 2 * g)
                z = bank[4 + g % 2]
                for t in range(GT):
                    scale = dis[:, g * GT + t:g * GT + t + 1]
                    nc.scalar.activation(tmpA[:, t * P:(t + 1) * P], z[:, t * P:(t + 1) * P], ACT.Relu, scale=scale)
                    last = nc.scalar.activation(tmpB[:, t * P:(t + 1) * P], z[:, t * P:(t + 1) * P], ACT.Exp,
                                                scale=scale)
                last.then_inc(elu_parts, 1)

            def tokens_out(l, g):
                act.wait_ge(stats_ready[l], g + 1)
                for t in range(g * GT, (g + 1) * GT):
                    last = nc.scalar.activation(xmoe[:, t, 0:D], xres[:, t, :], ACT.Identity,
                                                bias=shift[:, t:t + 1], scale=rstd[:, t:t + 1])
                last.then_inc(xn_ready[l], 1)

            def xnT_out(l, g):
                act.wait_ge(xn_turned[l], g + 1)
                if g >= 2:
                    act.wait_ge(logits_done[l], g - 1)
                nc.scalar.copy(xnT[g % 2], bank[6 + g % 2][:]).then_inc(xnT_ready[l], 1)

            def after_aggregation(l):
                for s in range(NG + 2):
                    if s < NG:
                        aggregated_out(l, s)
                        elu_halves(l, s)
                    if 1 <= s <= NG:
                        tokens_out(l, s - 1)
                        xnT_out(l, s - 1)
                act.wait_ge(gap_ready[l], NG)
                nc.scalar.activation(gap[:], gap[:], ACT.Exp).then_inc(gap_exp[l], 1)

            def filter_piece(k, a):
                act.wait_ge(squared, k + 1)
                nc.scalar.activation(a, a, ACT.Tanh).then_inc(filtered, 1)

            after_aggregation(0)
            for g in range(NG):
                act.wait_ge(gates_turned, g + 1)
                if g >= 2:
                    act.wait_ge(bias_done, g - 1)
                nc.scalar.copy(wide[0:E, g % 2, :], bank[4 + g % 2][0:E, :]).then_inc(gatesT_ready, 1)

            def up_weights(l, i, h, expert):
                w = L0_ffn_w1.rearrange("e d f -> d e f") if l == 0 else w12_1.rearrange("p e w f -> p e (w f)")
                act.dma_start(up_w[l][:, h:h + 1, :], w[:, bass.ds(expert, 1), :]).then_inc(up_w_in[l][h], 16)

            def first_up_weights(l):
                first = window(slot_expert, ENG.Activation, 0, 0, UP, E - 1)
                for s in range(UP):
                    up_weights(l, 0, s, first[s])

            def row_to_send(s, lo, i, h):
                ri, rh = rounds(i, h, DOWN)
                act.wait_ge(down_done[1], s - DOWN + 1)
                if lo - DOWN >= RING:
                    act.wait_ge(row_out[1][rh], 16 * ri)
                nc.scalar.copy(slot_out[:, rh, :], bank[6 + (h - DOWN) % 2][:, 0:D]).then_inc(out_ready[1], 1)

            def step0(s, lo, hi, i, h, experts):
                if live(lo, hi, UP):
                    b = (h - UP) % 2
                    act.wait_ge(up_done[0], s - UP + 1)
                    if lo - UP >= 2:
                        act.wait_ge(down_done[0], s - UP - 1)
                    for f in range(FH):
                        last = nc.scalar.activation(hidT[:, b, f * P:(f + 1) * P], bank[2 + b][:, f * P:(f + 1) * P],
                                                    ACT.Relu, bias=b1T[:, f, bass.ds(experts[0], 1)])
                    last.then_inc(hidT_ready[0], 1)
                if live(lo, hi, -UP):
                    up_weights(0, *rounds(i, h, -UP), experts[RING])
                if lo >= FILTER_FROM and hi < FILTER_TO:
                    filter_piece(s - FILTER_FROM, piece(s - FILTER_FROM))

            act.wait_ge(slots_known[0], 1)
            fl = act.value_load(flag[0:1, 0:1], min_val=0, max_val=N)
            act.wait_ge(b1_ready, 1)
            more.append(is_beyond(act))
            first_up_weights(0)
            run_slots(act, step0, DOWN, lambda s: window(slot_expert, ENG.Activation, s, -UP, UNROLL + UP, E - 1))


            def one_more0(s, k):
                expert, = window(slot_expert, ENG.Activation, s, 0, 1, E - 1)
                act.wait_ge(x_up_done, k + 1)
                for f in range(FH):
                    last = nc.scalar.activation(hidT[:, 0, f * P:(f + 1) * P], bank[2][:, f * P:(f + 1) * P],
                                                ACT.Relu, bias=b1T[:, f, bass.ds(expert, 1)])
                last.then_inc(x_hidT_ready, 1)

            beyond_main(act, more, one_more0)
            for k in range(LATE_PIECES):
                filter_piece(PIECES + k, late_piece(k))
            with act.If(fl > 0):
                with act.Fori(0, NT) as r:
                    act.wait_ge(exact_sq, r + 1)
                    nc.scalar.activation(exact, exact, ACT.Tanh).then_inc(exact_tanh, 1)

            for g in range(NG):
                act.wait_ge(xn1_scale, g + 1)
                for t in range(g * GT, (g + 1) * GT):
                    last = nc.scalar.activation(xagg[:, t, :], xres[:, t, :], ACT.Identity,
                                                bias=shift[:, t:t + 1], scale=rstd[:, t:t + 1])
                last.then_inc(xn1_ready, 1)
                act.wait_ge(xn1_turned, g + 1)
                nc.scalar.copy(wide[:, 0, :], bank[4][:]).then_inc(xn1T_ready, 1)
                act.wait_ge(proj_done, g + 1)
                nc.scalar.activation(wide[:, 1, :], bank[5][:], ACT.Tanh, bias=proj_b[:, 0:1]).then_inc(h2_ready, 1)
                act.wait_ge(feat_done, g + 1)
                nc.scalar.copy(xagg[:, g * GT:(g + 1) * GT, :],
                               bank[6][:, :].rearrange("p (a b) -> p a b", a=GT)).then_inc(feat_ready, 1)

            after_aggregation(1)

            def step1(s, lo, hi, i, h, experts):
                if live(lo, hi, DOWN):
                    row_to_send(s, lo, i, h)
                if live(lo, hi, UP):
                    b = (h - UP) % 2
                    act.wait_ge(up_done[1], s - UP + 1)
                    if lo - UP >= 2:
                        act.wait_ge(hidT_ready[1], s - UP - 1)
                    nc.scalar.activation(silu[:, b, :], bank[2 + b][:, 0:F], ACT.Silu).then_inc(silu_ready, 1)
                if live(lo, hi, -UP):
                    up_weights(1, *rounds(i, h, -UP), experts[0])

            act.wait_ge(slots_known[1], 1)
            act.wait_ge(all_up_w_in, 16 * 2)
            more.append(is_beyond(act))
            first_up_weights(1)
            run_slots(act, step1, DOWN, lambda s: window(slot_expert, ENG.Activation, s, UP, UNROLL + UP, E - 1))

            def one_more1(s, k):
                act.wait_ge(x_up_done, k + 1)
                nc.scalar.activation(silu[:, 0, :], bank[2][:, 0:F], ACT.Silu).then_inc(x_silu, 1)
                act.wait_ge(x_down_done, k + 1)
                nc.scalar.copy(slot_out[:, 0, :], bank[6][:, 0:D]).then_inc(x_out_ready, 1)

            beyond_main(act, more, one_more1)

        @block.vector
        def _(dve):
            more = []
            V = nc.vector
            steps = Count(dve, dve_step)

            def run(ins):
                steps.inc(ins)
                steps.wait()

            def rsqrt(y, v, add):
                run(V.tensor_scalar(root_v[:], v, add, None, ALU.add))
                run(V.tensor_scalar(y.bitcast(i32), root_v[:, :].bitcast(i32), -0.5, float(0x5F3759DF),
                                    ALU.mult, ALU.add))
                for _ in range(3):
                    run(V.tensor_tensor(root_t[:], y, y, ALU.mult))
                    run(V.scalar_tensor_tensor(out=root_t[:], in0=root_t[:], scalar=-0.5, in1=root_v[:],
                                               op0=ALU.mult, op1=ALU.mult))
                    run(V.scalar_tensor_tensor(out=y, in0=root_t[:], scalar=1.5, in1=y,
                                               op0=ALU.add, op1=ALU.mult))

            def layer_stats(src, t0, signal=None):
                for t in range(GT):
                    steps.inc(V.bn_stats(stats[:, t, :], src[:, t0 + t, :]))
                steps.wait()
                for t in range(GT):
                    last = V.bn_aggr(mv[:, t0 + t, :], stats[:, t, :])
                    if signal is None or t < GT - 1:
                        steps.inc(last)
                    else:
                        last.then_inc(signal, 1)
                steps.wait()
                if signal is not None:
                    dve.wait_ge(signal, t0 // GT + 1)

            def scaled_tokens(g):
                dve.wait_ge(xs_scale, g + 1)
                for t in range(g * GT, (g + 1) * GT):
                    last = V.tensor_scalar(xagg[:, t, :], xres[:, t, :], rstd[:, t:t + 1], shift[:, t:t + 1],
                                           ALU.mult, ALU.add)
                last.then_inc(xs_ready, 1)

            dve.wait_ge(x_in, 16)
            layer_stats(xres, 0, input_stats_ready)

            for g in range(NG):
                for r in range(RING):
                    t = g * RING + r
                    dve.wait_ge(nat_in[r], (g + 1) * 16)
                    V.tensor_scalar(junkV, nat[:, r, :], 0.0, 0.0, ALU.is_gt, ALU.add,
                                    accum_out=nnz[:, t:t + 1]).then_inc(nnz_ready, 1)
                    for q in (0, 1):
                        dve.wait_ge(adj_turned, t * GT + q + 1)
                        V.tensor_copy(adjT[:, q * GT:(q + 1) * GT, t * P:(t + 1) * P],
                                      bank[4 + q][:, :].rearrange("p (a b) -> p a b", a=GT)).then_inc(adjT_dve, 1)
                    dve.wait_ge(nnz_ready, t + 1)
                    if g >= 1 and r == 0:
                        scaled_tokens(g - 1)
                if g < NG - 1:
                    layer_stats(xres, (g + 1) * GT, input_stats_ready)
            scaled_tokens(NG - 1)

            run(V.tensor_scalar(over[:], nnz[:], float(TOP), None, ALU.is_gt))
            steps.inc(V.tensor_reduce(over_any[:], over[:], AX, ALU.max))
            dve.wait_ge(b1_turned, 1)
            V.tensor_copy(b1T[:, :, :], bank[4][:, 0:FH * E].rearrange("p (f e) -> p f e", f=FH)).then_inc(b1_ready, 1)

            def graph_to_residual(l, g):
                t0 = g * GT
                xg = xres[:, t0:t0 + GT, :]
                z = bank[4 + g % 2][:, :].rearrange("p (t d) -> p t d", t=GT)
                if l == 1:
                    dve.wait_ge(z_done[l], g + 1)
                    V.tensor_tensor(xg, z, xg, ALU.add).then_inc(z_used, 1)
                    dve.wait_ge(z_used, g + 1)
                    return
                dve.wait_ge(elu_parts, g + 1)
                V.scalar_tensor_tensor(out=tmpA, in0=tmpB, scalar=1.0, in1=tmpA, op0=ALU.min,
                                       op1=ALU.add).then_inc(elu_used, 1)
                dve.wait_ge(elu_used, 2 * g + 1)
                V.scalar_tensor_tensor(out=xg, in0=tmpA.rearrange("p (t d) -> p t d", t=GT), scalar=-1.0, in1=xg,
                                       op0=ALU.add, op1=ALU.add).then_inc(elu_used, 1)
                dve.wait_ge(elu_used, 2 * g + 2)

            def gate_group(l, g):
                t0 = g * GT
                dve.wait_ge(logits_done[l], g + 1)
                run(V.tensor_tensor(logits, bank[g][:, 0:GT * E].rearrange("p (t e) -> p t e", t=GT),
                                    gate_b[l][:, :].unsqueeze(1).to_broadcast([P, GT, E]), ALU.add))
                for t in range(GT):
                    steps.inc(V.max(out=top[:, t, :], in_=logits[:, t, :]))
                steps.wait()
                for t in range(GT):
                    steps.inc(V.max_index(out=topi[:, t, :], in_max=top[:, t, :], in_values=logits[:, t, :]))
                steps.wait()
                steps.inc(V.tensor_copy(chosen[:, :, t0:t0 + GT], topi[:, :, 0:K].rearrange("p t k -> p k t")))
                steps.wait()
                for k in range(K):
                    V.tensor_tensor(onehot[:, :, k, :], iota_e[:, :].unsqueeze(2).to_broadcast([P, E, GT]),
                                    chosen[:, k, t0:t0 + GT].unsqueeze(1).to_broadcast([P, E, GT]),
                                    ALU.is_equal).then_inc(onehot_ready[l], 1)
                V.tensor_tensor(gap[:, t0:t0 + GT], top[:, :, 1], top[:, :, 0], ALU.subtract).then_inc(gap_ready[l], 1)
                steps.inc(V.tensor_tensor(xmoe[:, t0:t0 + GT, D + 1], chosen[:, 0, t0:t0 + GT],
                                          chosen[:, 1, t0:t0 + GT], ALU.max))

            def rank_group(l, g):
                t0 = g * GT
                later, counts = bank[g][:, 128:128 + EC], bank[g][:, 256:256 + EC]
                dve.wait_ge(ranks_done[l], g + 1)
                dve.wait_ge(onehot_ready[l], K * (g + 1))
                steps.inc(V.tensor_tensor_scan(running, segment[:], counts, 0.0, ALU.mult, ALU.add))
                run(V.tensor_tensor(by_expert, later.rearrange("p (e c) -> p e c", c=C),
                                    base[:, :].unsqueeze(2).to_broadcast([P, E, C]), ALU.add))
                steps.inc(V.tensor_tensor(base[:], running.rearrange("p (e c) -> p e c", c=C)[:, :, C - 1],
                                          base[:], ALU.add))
                run(V.tensor_tensor(tile_rank, tile_rank, running, ALU.add))
                run(V.tensor_tensor(tile_rank, tile_rank, onehot.rearrange("p e k t -> p (e k t)"), ALU.mult))
                run(V.tensor_reduce(pos_f, tile_rank.rearrange("p (e c) -> p c e", c=C), AX, ALU.add))
                V.tensor_copy(pos[:, :, t0:t0 + GT], pos_f.rearrange("p (k t) -> p k t", k=K)).then_inc(routed[l], 1)

            def after_aggregation(l):
                run(V.tensor_copy(base[:], base0[:]))
                for s in range(NG + 1):
                    if s < NG:
                        t0 = s * GT
                        graph_to_residual(l, s)
                        layer_stats(xres, t0)
                        rsqrt(rstd[:, t0:t0 + GT], mv[:, t0:t0 + GT, 1], EPS)
                        V.scalar_tensor_tensor(out=shift[:, t0:t0 + GT], in0=mv[:, t0:t0 + GT, 0], scalar=-1.0,
                                               in1=rstd[:, t0:t0 + GT], op0=ALU.mult,
                                               op1=ALU.mult).then_inc(stats_ready[l], 1)
                    if s >= 1:
                        gate_group(l, s - 1)
                        rank_group(l, s - 1)

            def plan_slots(l):
                run(V.tensor_tensor(slots_f[:], base[:], base0[:], ALU.subtract))
                run(V.tensor_copy(count_i[:], slots_f[:]))
                run(V.tensor_scalar(count_i[:], count_i[:], P - 1, None, ALU.add))
                run(V.tensor_scalar(count_i[:], count_i[:], P.bit_length() - 1, None, ALU.arith_shift_right))
                run(V.tensor_copy(slots_f[:], count_i[:]))
                run(V.tensor_tensor_scan(slots_end[:], ones[:, 0:E], slots_f[:], 0.0, ALU.mult, ALU.add))
                for half in range(2):
                    part = slice(half * E // 2, (half + 1) * E // 2)
                    steps.inc(V.tensor_tensor(ends[half], slots_end[:, part].unsqueeze(1).to_broadcast([P, SLOTS, E // 2]),
                                              iota_s[:, :].unsqueeze(2).to_broadcast([P, SLOTS, E // 2]), ALU.is_le))
                steps.wait()
                for half in range(2):
                    steps.inc(V.tensor_reduce(se_half[half], ends[half], AX, ALU.add))
                steps.wait()
                for half in range(2):
                    part = slice(half * E // 2, (half + 1) * E // 2)
                    steps.inc(V.tensor_tensor(ends[half], ends[half],
                                              slots_f[:, part].unsqueeze(1).to_broadcast([P, SLOTS, E // 2]), ALU.mult))
                steps.wait()
                for half in range(2):
                    steps.inc(V.tensor_reduce(start_f[half], ends[half], AX, ALU.add))
                run(V.tensor_tensor(se_f[:], se_half[0], se_half[1], ALU.add))
                run(V.tensor_tensor(start_f[0], start_f[0], start_f[1], ALU.add))
                run(V.tensor_tensor(start_f[0], iota_s[:], start_f[0], ALU.subtract))
                steps.inc(V.tensor_scalar(row_f, se_f[:], float(RUN), None, ALU.mult))
                steps.wait()
                run(V.scalar_tensor_tensor(out=row_f, in0=start_f[0], scalar=float(P), in1=row_f,
                                           op0=ALU.mult, op1=ALU.add))
                run(V.tensor_scalar(row_f, row_f, base[:, E - 1:E], None, ALU.min))
                run(V.tensor_scalar(se_f[:], se_f[:], float(E - 1), None, ALU.min))
                run(V.tensor_copy(slot_row[0:1, LEAD:LEAD + SLOTS], row_f[0:1, :]))
                run(V.tensor_scalar(beyond[0:1, 0:1], slots_end[0:1, E - 1:E], float(MAIN), None, ALU.is_gt))
                V.tensor_copy(slot_expert[0:1, LEAD:LEAD + SLOTS], se_f[0:1, :]).then_inc(slots_known[l], 1)

            def runs_and_weights(l):
                V.tensor_copy(run_end[0:1, :], base[0:1, :]).then_inc(runs_known[l], 1)
                dve.wait_ge(gap_exp[l], 1)
                run(V.tensor_scalar(wsum[:], gap[:], 1.0, None, ALU.add))
                run(V.reciprocal(wk[:, 0, :], wsum[:]))
                run(V.tensor_tensor(wk[:, 1, :], wk[:, 0, :], gap[:], ALU.mult))
                steps.inc(V.tensor_tensor(swap[:, 0, :], chosen[:, 0, :], chosen[:, 1, :], ALU.is_gt))
                steps.inc(V.tensor_tensor(swap[:, 1, :], chosen[:, 0, :], chosen[:, 1, :], ALU.is_le))
                steps.wait()
                for k in range(K):
                    run(V.tensor_tensor(wsum[:], swap[:, 1 - k, :], wk[:, 0, :], ALU.mult))
                    run(V.tensor_tensor(wrow[:, k, :], swap[:, k, :], wk[:, 1, :], ALU.mult))
                    run(V.tensor_tensor(wrow[:, k, :], wrow[:, k, :], wsum[:], ALU.add))

            def square_piece(a):
                V.scalar_tensor_tensor(out=a, in0=a, scalar=0.0, in1=a, op0=ALU.max,
                                       op1=ALU.mult).then_inc(squared, 1)

            def combine(l, g, acc):
                dve.wait_ge(tok_in[l][g], 16)
                for k in range(K):
                    for t in range(g * GT, (g + 1) * GT):
                        last = V.scalar_tensor_tensor(out=acc[:, t, :], in0=tok[l][:, t, k, :],
                                                      scalar=wrow[:, k, t:t + 1], in1=acc[:, t, :],
                                                      op0=ALU.mult, op1=ALU.add)
                        if k == K - 1 and t == (g + 1) * GT - 1:
                            last.then_inc(combined[l], 1)
                        else:
                            steps.inc(last)
                    if k == 0:
                        steps.wait()
                steps.wait()
                dve.wait_ge(combined[l], g + 1)

            after_aggregation(0)
            dve.wait_ge(ranks_done[0], NG)
            steps.inc(V.tensor_copy(flag[0:1, 0:1], bank[3][0:1, 400:401]))
            runs_and_weights(0)
            for k in range(K):
                run(V.tensor_tensor(gates_k, iota_e[:, :].unsqueeze(1).to_broadcast([P, NT, E]),
                                    chosen[:, k, :].unsqueeze(2).to_broadcast([P, NT, E]), ALU.is_equal))
                if k == 0:
                    run(V.tensor_tensor(gates, gates_k, wk[:, k, :].unsqueeze(2).to_broadcast([P, NT, E]), ALU.mult))
                else:
                    run(V.tensor_tensor(gates_k, gates_k, wk[:, k, :].unsqueeze(2).to_broadcast([P, NT, E]), ALU.mult))
                    V.tensor_tensor(gates, gates, gates_k, ALU.add).then_inc(gates_ready, 1)
            dve.wait_ge(gates_ready, 1)
            plan_slots(0)
            for g in range(NG):
                dve.wait_ge(bias_done, g + 1)
                V.tensor_tensor(xagg[:, g * GT:(g + 1) * GT, :], bank[g][:, :].rearrange("p (t d) -> p t d", t=GT),
                                xmoe[:, g * GT:(g + 1) * GT, 0:D], ALU.add).then_inc(bias_used, 1)

            def row_to_send(s, lo, i, h):
                ri, rh = rounds(i, h, DOWN)
                dve.wait_ge(down_done[0], s - DOWN + 1)
                if lo - DOWN >= RING:
                    dve.wait_ge(row_out[0][rh], 16 * ri)
                V.tensor_copy(slot_out[:, rh, :], bank[6 + (h - DOWN) % 2][:, 0:D]).then_inc(out_ready[0], 1)

            def row_arrived(l, s, lo, i, h):
                dve.wait_ge(row_turned[l], s + 1)
                V.tensor_copy(slotT[:, h % 2, :], bank[h % 2][:, 0:P]).then_inc(rowT_ready[l], 1)
                dve.wait_ge(row_in[l][h], 16 * (i + 1))
                V.scalar_tensor_tensor(out=early[:, bass.ds(s, 1)], in0=slot_in[:, h, D + 1:D + 2],
                                       scalar=se_f[:, bass.ds(s, 1)], in1=slot_in[:, h, D:D + 1],
                                       op0=ALU.is_equal, op1=ALU.add).then_inc(early_ready[l], 1)

            def step0(s, lo, hi, i, h, _):
                if live(lo, hi, DOWN):
                    row_to_send(s, lo, i, h)
                if live(lo, hi, 0):
                    row_arrived(0, s, lo, i, h)
                if lo >= FILTER_FROM and hi < FILTER_TO:
                    square_piece(piece(s - FILTER_FROM))

            def row_beyond(l, s, k):
                dve.wait_ge(x_row_turned, k + 1)
                V.tensor_copy(slotT[:, 0, :], bank[0][:, 0:P]).then_inc(x_rowT_ready, 1)
                dve.wait_ge(x_row_in, 16 * (k + 1))
                V.scalar_tensor_tensor(out=early[:, bass.ds(s, 1)], in0=slot_in[:, 0, D + 1:D + 2],
                                       scalar=se_f[:, bass.ds(s, 1)], in1=slot_in[:, 0, D:D + 1],
                                       op0=ALU.is_equal, op1=ALU.add).then_inc(x_early, 1)

            def one_more0(s, k):
                row_beyond(0, s, k)
                dve.wait_ge(x_down_done, k + 1)
                V.tensor_copy(slot_out[:, 0, :], bank[6][:, 0:D]).then_inc(x_out_ready, 1)

            dve.wait_ge(slots_known[0], 1)
            fl = dve.value_load(flag[0:1, 0:1], min_val=0, max_val=N)
            more.append(is_beyond(dve))
            run_slots(dve, step0, DOWN)
            beyond_main(dve, more, one_more0)
            for k in range(LATE_PIECES):
                square_piece(late_piece(k))
            with dve.If(fl > 0):
                dve.wait_ge(filtered, PIECES + LATE_PIECES)
                rounds_full, rest = TOP // 8, TOP % 8
                V.memset(over[:, 0:1], 0.0).then_inc(exact_used, 1)
                with dve.Fori(0, NT) as r:
                    per = 3 + 2 * rounds_full + 3
                    k = [0]

                    def chained(ins):
                        ins.then_inc(exact_step, 1)
                        k[0] += 1
                        dve.wait_ge(exact_step, r * per + k[0])
                        V.memset(over[:, 1:2], 0.0)

                    dve.wait_ge(exact_in, (r + 1) * 16)
                    V.scalar_tensor_tensor(out=exact, in0=exact, scalar=0.0, in1=exact, op0=ALU.max,
                                           op1=ALU.mult).then_inc(exact_sq, 1)
                    dve.wait_ge(exact_tanh, r + 1)
                    chained(V.tensor_copy(remain[:, 0:N], exact))
                    chained(V.memset(remain[:, N:N + 8], -1.0))
                    for _ in range(rounds_full):
                        chained(V.max(out=top8, in_=remain))
                        chained(V.match_replace(out=remain, in_to_replace=top8, in_values=remain, imm_value=0.0))
                    chained(V.max(out=top8, in_=remain))
                    chained(V.memset(top8[:, rest:8], -1.0))
                    chained(V.match_replace(out=remain, in_to_replace=top8, in_values=remain, imm_value=0.0))
                    chained(V.tensor_tensor(remain[:, 0:N], exact, remain[:, 0:N], ALU.subtract))
                    assert k[0] == per
                    for q in range(GT):
                        dve.wait_ge(exact_turned, r * GT + q + 1)
                        V.tensor_copy(adjT[:, q * GT:(q + 1) * GT, bass.ds(r * P, P)],
                                      bank[4 + q % 2][:, :].rearrange("p (a b) -> p a b", a=GT)).then_inc(exact_kept, 1)
                    dve.wait_ge(exact_kept, (r + 1) * GT)
                    V.memset(over[:, 0:1], 0.0).then_inc(exact_used, 1)

            for g in range(NG):
                combine(0, g, xagg)
                layer_stats(xagg, g * GT, mix_stats)
                for t in range(g * GT, (g + 1) * GT):
                    steps.inc(V.scalar_tensor_tensor(out=xagg[:, t, :], in0=xagg[:, t, :], scalar=mv[:, t, 0:1],
                                                     in1=gamma[:], op0=ALU.subtract, op1=ALU.mult))
                steps.wait()
                dve.wait_ge(mix_scale, g + 1)
                for t in range(g * GT, (g + 1) * GT):
                    steps.inc(V.scalar_tensor_tensor(out=xres[:, t, :], in0=xagg[:, t, :], scalar=rstd[:, t:t + 1],
                                                     in1=xres[:, t, :], op0=ALU.mult, op1=ALU.add))
                steps.wait()
                layer_stats(xres, g * GT, xn1_stats)

            after_aggregation(1)
            runs_and_weights(1)
            plan_slots(1)

            def step1(s, lo, hi, i, h, _):
                if live(lo, hi, UP):
                    b = (h - UP) % 2
                    dve.wait_ge(silu_ready, s - UP + 1)
                    if lo - UP >= 2:
                        dve.wait_ge(down_done[1], s - UP - 1)
                    V.tensor_tensor(hidT[:, b, :], silu[:, b, :], bank[2 + b][:, F:2 * F],
                                    ALU.mult).then_inc(hidT_ready[1], 1)
                if live(lo, hi, 0):
                    row_arrived(1, s, lo, i, h)

            def one_more1(s, k):
                row_beyond(1, s, k)
                dve.wait_ge(x_silu, s - (MAIN - 1))
                V.tensor_tensor(hidT[:, 0, :], silu[:, 0, :], bank[2][:, F:2 * F],
                                ALU.mult).then_inc(x_hidT_ready, 1)

            dve.wait_ge(slots_known[1], 1)
            more.append(is_beyond(dve))
            run_slots(dve, step1, UP)
            beyond_main(dve, more, one_more1)
            for g in range(NG):
                combine(1, g, xres)

        @block.tensor
        def _(pe):
            more = []
            T = nc.tensor
            pe.wait_ge(consts, 1)

            def products(g, tiles, first, last):
                return [lambda j=j: T.matmul(bank[g][:], xagg[:, j, :], adjT[:, j, g * GW:(g + 1) * GW],
                                             start=(j == first), stop=(j == last)) for j in tiles]

            def adj_rows(g, beside):
                for r in range(RING):
                    t = g * RING + r
                    pe.wait_ge(nat_in[r], (g + 1) * 16)
                    for q in range(GT):
                        if t >= 1:
                            pe.wait_ge(adjT_dve if q < 2 else adjT_act, 2 * (t - 1) + q % 2 + 1)
                        for b in range(GT):
                            last = T.transpose(bank[4 + q][:, b * P:(b + 1) * P],
                                               nat[:, r, (q * GT + b) * P:(q * GT + b + 1) * P], ident[:])
                        last.then_inc(adj_turned, 1)
                        at = r * GT + q
                        if at == GT and beside:
                            all_in(g - 1)
                        if at >= GT:
                            steps = GT * (RING - 1)
                            for go in beside[(at - GT) * len(beside) // steps:(at - GT + 1) * len(beside) // steps]:
                                go()

            def all_in(g):
                pe.wait_ge(adjT_dve, 2 * (g + 1) * RING)
                pe.wait_ge(adjT_act, 2 * (g + 1) * RING)
                pe.wait_ge(xs_ready, g + 1)

            beside = []
            for g in range(NG):
                adj_rows(g, beside)
                beside = [go for i in range(g + 1)
                          for go in products(i, range(0 if i == g else g * GT, (g + 1) * GT), 0, NT)]
            all_in(NG - 1)

            def to_token_major(l, g):
                pe.wait_ge(agg_out[l], g + 1)
                if g >= 2 and l == 0:
                    pe.wait_ge(elu_parts, g - 1)
                if g >= 2 and l == 1:
                    pe.wait_ge(z_used, g - 1)
                for b in range(GT):
                    o, a = bank[4 + g % 2][:, b * P:(b + 1) * P], wide[:, g % 2, b * P:(b + 1) * P]
                    last = T.matmul(o, a, gnn_w[:], start=True, stop=True) if l == 0 else T.transpose(o, a, ident[:])
                last.then_inc(z_done[l], 1)

            def turn_tokens(l, g):
                pe.wait_ge(xn_ready[l], g + 1)
                if g >= 2:
                    pe.wait_ge(xnT_ready[l], g - 1)
                for b in range(GT):
                    last = T.transpose(bank[6 + g % 2][:, b * P:(b + 1) * P], xmoe[:, g * GT + b, 0:D], ident[:])
                last.then_inc(xn_turned[l], 1)

            def gate_logits(l, g):
                pe.wait_ge(xnT_ready[l], g + 1)
                for b in range(GT):
                    last = T.matmul(bank[g][:, b * E:(b + 1) * E], xnT[g % 2][:, b * P:(b + 1) * P], gate_w[l][:],
                                    start=True, stop=True)
                last.then_inc(logits_done[l], 1)

            def count_ranks(l, g):
                m = onehot.rearrange("p e k t -> p (e k t)")
                pe.wait_ge(onehot_ready[l], K * (g + 1))
                T.matmul(bank[g][:, 128:128 + EC], not_before[:], m, start=True, stop=True)
                if l == 0 and g == NG - 1:
                    T.matmul(bank[g][:, 400:401], ones[:], over_any[:], start=True, stop=True)
                T.matmul(bank[g][:, 256:256 + EC], ones[:], m, start=True, stop=True).then_inc(ranks_done[l], 1)

            def graph_layer_end(l, between):
                done, todo = 0, []
                for g in range(NG):
                    tiles = range(0 if l == 0 and g == NG - 1 else NT - (2 * GT if l == 1 and g >= 2 else GT), NT)
                    todo += [(g, go, j == tiles[-1]) for j, go in zip(tiles, products(g, tiles, 0, NT - 1))]

                def until(n):
                    nonlocal done
                    for g, go, last in todo[done:n]:
                        if last and l == 0:
                            for b in range(GT):
                                T.matmul(bank[g][:, b * P:(b + 1) * P], xagg[:, g * GT + b, :], ident[:],
                                         start=False, stop=False)
                        product = go()
                        if last:
                            product.then_inc(agg_done[l], 1)
                    done = max(done, n)

                for n, step, g in between:
                    until(n)
                    step(l, g)
                until(len(todo))
                to_token_major(l, 3)
                count_ranks(l, 1)
                for g in (2, 3):
                    turn_tokens(l, g)
                    gate_logits(l, g)
                    count_ranks(l, g)

            held_flag = []

            def slots(l):
                w_down = w2_0 if l == 0 else w3_1
                up = F if l == 0 else 2 * F

                def step(s, lo, hi, i, h, experts):
                    if live(lo, hi, DOWN):
                        b = (h - DOWN) % 2
                        pe.wait_ge(hidT_ready[l], s - DOWN + 1)
                        if lo - DOWN >= 2:
                            pe.wait_ge(out_ready[l], s - DOWN - 1)
                        for f in range(FH):
                            last = T.matmul(bank[6 + b][:, 0:D], hidT[:, b, f * P:(f + 1) * P],
                                            w_down[:, bass.ds(experts[0], 1), f, :],
                                            start=(f == 0), stop=(f == FH - 1))
                        last.then_inc(down_done[l], 1)
                    if live(lo, hi, UP):
                        b, (ri, rh) = (h - UP) % 2, rounds(i, h, UP)
                        pe.wait_ge(rowT_ready[l], s - UP + 1)
                        pe.wait_ge(up_w_in[l][rh], 16 * (ri + 1))
                        if lo - UP >= 2:
                            pe.wait_ge(hidT_ready[l], s - UP - 1)
                        for f in range(up // P):
                            last = T.matmul(bank[2 + b][:, f * P:(f + 1) * P],
                                            up_w[l][:, rh, f * P:(f + 1) * P], slotT[:, b, :],
                                            start=True, stop=True)
                        last.then_inc(up_done[l], 1)
                    if live(lo, hi, 0):
                        pe.wait_ge(row_in[l][h], 16 * (i + 1))
                        if lo >= 2:
                            pe.wait_ge(rowT_ready[l], s - 1)
                        T.transpose(bank[h % 2][:, 0:P], slot_in[:, h, 0:D], ident[:]).then_inc(row_turned[l], 1)

                pe.wait_ge(slots_known[l], 1)
                if l == 0:
                    pe.wait_ge(bias_used, NG)
                pe.wait_ge(down_w_in[l], 16)
                if l == 0:
                    held_flag.append(pe.value_load(flag[0:1, 0:1], min_val=0, max_val=N))
                more.append(is_beyond(pe))
                run_slots(pe, step, DOWN, lambda s: window(slot_expert, ENG.PE, s, -DOWN, UNROLL - DOWN, E - 1))

                def one_more(s, k):
                    expert, = window(slot_expert, ENG.PE, s, 0, 1, E - 1)
                    pe.wait_ge(x_row_in, 16 * (k + 1))
                    T.transpose(bank[0][:, 0:P], slot_in[:, 0, 0:D], ident[:]).then_inc(x_row_turned, 1)
                    pe.wait_ge(x_rowT_ready, k + 1)
                    pe.wait_ge(x_up_w_in, 16 * (k + 1))
                    for f in range(up // P):
                        last = T.matmul(bank[2][:, f * P:(f + 1) * P], up_w[l][:, 0, f * P:(f + 1) * P],
                                        slotT[:, 0, :], start=True, stop=True)
                    last.then_inc(x_up_done, 1)
                    pe.wait_ge(x_hidT_ready, k + 1)
                    for f in range(FH):
                        last = T.matmul(bank[6][:, 0:D], hidT[:, 0, f * P:(f + 1) * P],
                                        w_down[:, bass.ds(expert, 1), f, :], start=(f == 0), stop=(f == FH - 1))
                    last.then_inc(x_down_done, 1)

                beyond_main(pe, more, one_more)

            pe.wait_ge(small_in, 16 * SMALL_LOADS)
            for f in range(FH):
                last = T.transpose(bank[4][:, f * E:(f + 1) * E], b1_rows[:, f * P:(f + 1) * P], ident[0:E, 0:E])
            last.then_inc(b1_turned, 1)
            pe.wait_ge(b1_ready, 1)
            graph_layer_end(0, [
                (6, to_token_major, 0), (10, to_token_major, 1), (16, turn_tokens, 0), (17, gate_logits, 0),
                (17, to_token_major, 2), (20, count_ranks, 0), (21, turn_tokens, 1), (22, gate_logits, 1)])
            for g in range(NG + 1):
                if g < NG:
                    pe.wait_ge(gates_ready, 1)
                    if g >= 2:
                        pe.wait_ge(gatesT_ready, g - 1)
                    for b in range(GT):
                        last = T.matmul(bank[4 + g % 2][0:E, b * P:(b + 1) * P], gates[:, g * GT + b, :], ident[:],
                                        start=True, stop=True)
                    last.then_inc(gates_turned, 1)
                if g >= 1:
                    pe.wait_ge(gatesT_ready, g)
                    for b in range(GT):
                        last = T.matmul(bank[g - 1][:, b * P:(b + 1) * P],
                                        wide[0:E, (g - 1) % 2, b * P:(b + 1) * P], b2[:], start=True, stop=True)
                    last.then_inc(bias_done, 1)
            slots(0)

            with pe.If(held_flag[0] > 0):
                with pe.Fori(0, NT) as r:
                    pe.wait_ge(exact_step, (r + 1) * (3 + 2 * (TOP // 8) + 3))
                    for q in range(GT):
                        if q >= 2:
                            pe.wait_ge(exact_kept, r * GT + q - 1)
                        for b in range(GT):
                            last = T.transpose(bank[4 + q % 2][:, b * P:(b + 1) * P],
                                               remain[:, (q * GT + b) * P:(q * GT + b + 1) * P], ident[:])
                        last.then_inc(exact_turned, 1)
                    pe.wait_ge(exact_kept, (r + 1) * GT)

            beside = []
            for g in range(NG):
                if g == NG - 1:
                    beside = beside[:2 * GT]
                third = (len(beside) + 1) // 3
                pe.wait_ge(xn1_ready, g + 1)
                for b in range(GT):
                    last = T.transpose(bank[4][:, b * P:(b + 1) * P], xagg[:, g * GT + b, :], ident[:])
                last.then_inc(xn1_turned, 1)
                for go in beside[:third]:
                    go()
                pe.wait_ge(xn1T_ready, g + 1)
                T.matmul(bank[5][:], proj_w[:], wide[:, 0, :], start=True, stop=True).then_inc(proj_done, 1)
                for go in beside[third:2 * third]:
                    go()
                pe.wait_ge(h2_ready, g + 1)
                for b in range(GT):
                    last = T.matmul(bank[6][:, b * P:(b + 1) * P], wide[:, 1, b * P:(b + 1) * P], gcn_w[:],
                                    start=True, stop=True)
                last.then_inc(feat_done, 1)
                for go in beside[2 * third:]:
                    go()
                if g == 0:
                    pe.wait_ge(filtered, PIECES + LATE_PIECES)
                pe.wait_ge(feat_ready, g + 1)
                beside = [go for i in range(NG) for go in products(i, range(g * GT, (g + 1) * GT), 0, NT - 1)]

            graph_layer_end(1, [
                (6, to_token_major, 0), (10, to_token_major, 1), (12, turn_tokens, 0), (13, gate_logits, 0),
                (16, count_ranks, 0), (18, to_token_major, 2), (18, turn_tokens, 1), (19, gate_logits, 1)])
            slots(1)


_INS = ['x', 'adj', 'L0_gnn_w', 'L0_ffn_gate_w', 'L0_ffn_gate_b', 'L0_ffn_w1', 'L0_ffn_b1', 'L0_ffn_w2', 'L0_ffn_b2',
        'L0_ffn_gamma', 'L0_ffn_beta', 'L1_gnn_W_proj', 'L1_gnn_b_proj', 'L1_gnn_W_gcn', 'L1_gnn_b_gcn',
        'L1_ffn_gate_w', 'L1_ffn_gate_b', 'L1_ffn_w1', 'L1_ffn_w2', 'L1_ffn_w3']
_OUTS = [((2048, 128), 'float32')]


def kernel(**inputs):
    import numpy as _np
    import concourse.bacc as _bacc
    from concourse import mybir as _mybir
    from concourse.bass_utils import run_bass_kernel_spmd as _run

    nc = _bacc.Bacc("TRN2", target_bir_lowering=False, num_devices=1)
    arrays, args = {}, []
    for name in _INS:
        a = _np.ascontiguousarray(inputs[name])
        arrays[f"in_{name}_dram"] = a
        args.append(nc.dram_tensor(f"in_{name}_dram", a.shape, _mybir.dt.from_np(a.dtype), kind="ExternalInput").ap())
    for i, (shape, dtype) in enumerate(_OUTS):
        dt = _mybir.dt.from_np(_np.dtype(dtype))
        args.append(nc.dram_tensor(f"out_{i}_dram", shape, dt, kind="ExternalOutput").ap())
    gnn_moe_gnn_moe_kernel(nc, *args)
    r = _run(nc, [arrays], core_ids=[0])
    return r.results[0]["out_0_dram"]
```
